# Optimizing a Trainium2 kernel written in Bass

```python
import numpy as np
import jax
import jax.numpy as jnp

def _softmax(x, axis=-1):
    return jax.nn.softmax(x, axis=axis)

def _gelu(x):
    return jax.nn.gelu(x, approximate=True)

def _silu(x):
    return jax.nn.silu(x)

def _sigmoid(x):
    return jax.nn.sigmoid(x)

def _layernorm(x, axis=-1, eps=1e-05):
    m = jnp.mean(x, axis=axis, keepdims=True)
    v = jnp.var(x, axis=axis, keepdims=True)
    return (x - m) / jnp.sqrt(v + eps)

def _scatter_add(tgt, idx, src, axis=0):
    return tgt.at[idx].add(src)

def _segment_sum(src, seg, n):
    return jax.ops.segment_sum(src, seg, n)
kernel_name = 'mk_adaln_ffn_d2_seqx_r2_0e5e32'

def setup_inputs(seed: int=0):
    np.random.seed(seed)
    _w = jnp.asarray

    def _rec_inputs():
        import jax
        import jax.numpy as jnp
        _rk = jax.random.key(seed)
        x = -7.109e-05 + 0.9999 * jax.random.normal(jax.random.fold_in(_rk, 1), (32, 128, 1024), jnp.float32)
        _lenS = 128 - jax.random.randint(jax.random.fold_in(_rk, 7), (32,), 0, max(1, 128 // 4) + 1, jnp.int32)
        _lenS2 = 128 - jax.random.randint(jax.random.fold_in(_rk, 8), (32,), 0, max(1, 128 // 4) + 1, jnp.int32)
        itok_B_1_198 = jax.random.randint(jax.random.fold_in(_rk, 11), (32,), 1, 199, jnp.int32)
        itok_B_0_6 = jax.random.randint(jax.random.fold_in(_rk, 12), (32,), 0, 7, jnp.int32)
        return (x, itok_B_1_198, itok_B_0_6)
    x, itok_B_1_198, itok_B_0_6 = _rec_inputs()

    def _L0_cond_setup():
        import jax, jax.numpy as jnp
        import numpy as np
        B, C, T = (128, 128, 1024)
        S, D = (200, 128)
        key = jax.random.key(seed)
        k1, k2, k3 = jax.random.split(key, 3)
        x = jax.random.normal(k1, (B, C, T), dtype=jnp.float32)
        conditions = jax.random.randint(k2, (B,), 0, S, dtype=jnp.int64)
        weights = jax.random.normal(k3, (S, C, D), dtype=jnp.float32) / jnp.sqrt(jnp.float32(C))
        return {'x': x, 'conditions': conditions, 'weights': weights}
    _L0_cond_all = _L0_cond_setup()
    _L0_cond_in = {k: v for k, v in _L0_cond_all.items() if k in ('weights',)}
    del _L0_cond_all

    def _L0_ffn_setup():
        import jax, jax.numpy as jnp
        import numpy as np
        E = 64
        K = 8
        H = 1024
        I = 384
        CAP = 256

        def _moe(hidden_states, gate_w, wg, wu, wd):
            B, S, Hd = hidden_states.shape
            x = hidden_states.reshape(-1, Hd)
            T = x.shape[0]
            logits = x @ gate_w.T
            probs = jax.nn.softmax(logits.astype(jnp.float32), axis=-1)
            w, sel = jax.lax.top_k(probs, K)
            w = w / jnp.sum(w, axis=-1, keepdims=True)
            w = w.astype(x.dtype)
            eid = sel.reshape(-1)
            tok = jnp.repeat(jnp.arange(T), K)
            oh = jax.nn.one_hot(eid, E, dtype=jnp.int32)
            pos = jnp.sum(jnp.cumsum(oh, axis=0) * oh, axis=-1) - 1
            valid = pos < CAP
            slot = jnp.where(valid, pos, CAP)
            xin = jnp.zeros((E, CAP + 1, Hd), x.dtype).at[eid, slot].set(x[tok])
            inp = xin[:, :CAP]
            h = jax.nn.silu(jnp.einsum('ech,ehi->eci', inp, wg)) * jnp.einsum('ech,ehi->eci', inp, wu)
            out = jnp.einsum('eci,eih->ech', h, wd)
            out_pad = jnp.concatenate([out, jnp.zeros((E, 1, Hd), out.dtype)], axis=1)
            g = out_pad[eid, slot] * (w.reshape(-1) * valid.astype(w.dtype))[:, None]
            y = jnp.zeros((T, Hd), x.dtype).at[tok].add(g)
            return y.reshape(B, S, Hd)
        key = jax.random.key(seed)
        k1, k2, k3, k4, k5 = jax.random.split(key, 5)
        hidden_states = jax.random.normal(k1, (1, 1024, H), dtype=jnp.float32)
        gate_w = jax.random.normal(k2, (E, H), dtype=jnp.float32) * 0.02
        wg = jax.random.normal(k3, (E, H, I), dtype=jnp.float32) * 0.02
        wu = jax.random.normal(k4, (E, H, I), dtype=jnp.float32) * 0.02
        wd = jax.random.normal(k5, (E, I, H), dtype=jnp.float32) * 0.02
        return {'hidden_states': hidden_states, 'gate_w': gate_w, 'wg': wg, 'wu': wu, 'wd': wd}
    _L0_ffn_all = _L0_ffn_setup()
    _L0_ffn_in = {k: v for k, v in _L0_ffn_all.items() if k in ('gate_w', 'wg', 'wu', 'wd')}
    del _L0_ffn_all

    def _L1_cond_setup():
        import jax, jax.numpy as jnp
        import numpy as np
        B, T, D_IN, D_OUT = (16, 1024, 1024, 1024)
        N_ADAPTERS, RANK = (8, 16)
        key = jax.random.key(seed)
        k_x, k_w, k_a, k_b, k_s, k_idx = jax.random.split(key, 6)
        x = jax.random.normal(k_x, (B, T, D_IN), dtype=jnp.float32)
        W = jax.random.normal(k_w, (D_OUT, D_IN), dtype=jnp.float32) * (1.0 / np.sqrt(D_IN))
        A = jax.random.normal(k_a, (N_ADAPTERS, RANK, D_IN), dtype=jnp.float32) * 0.02
        Bm = jax.random.normal(k_b, (N_ADAPTERS, D_OUT, RANK), dtype=jnp.float32) * 0.02
        scalings = jnp.ones((N_ADAPTERS,), dtype=jnp.float32)
        adapter_idx = jax.random.randint(k_idx, (B,), 0, N_ADAPTERS, dtype=jnp.int32)
        return {'x': x, 'W': W, 'A': A, 'Bm': Bm, 'scalings': scalings, 'adapter_idx': adapter_idx}
    _L1_cond_all = _L1_cond_setup()
    _L1_cond_in = {k: v for k, v in _L1_cond_all.items() if k in ('W', 'A', 'Bm', 'scalings')}
    del _L1_cond_all

    def _L1_ffn_setup():
        import jax, jax.numpy as jnp
        import numpy as np
        B, S, D_IN, D_OUT, E, R = (4, 1024, 1024, 1024, 8, 16)
        SCALING = 32.0 / 16.0
        key = jax.random.key(seed)
        ks = jax.random.split(key, 7)
        return {'x': jax.random.normal(ks[0], (B, S, D_IN), jnp.float32), 'base_w': jax.random.normal(ks[1], (D_OUT, D_IN), jnp.float32) * 0.02, 'base_b': jax.random.normal(ks[2], (D_OUT,), jnp.float32) * 0.02, 'router_w': jax.random.normal(ks[3], (E, D_IN), jnp.float32) * 0.02, 'router_b': jax.random.normal(ks[4], (E,), jnp.float32) * 0.02, 'lora_A': jax.random.normal(ks[5], (E, D_IN, R), jnp.float32) * 0.02, 'lora_B': jax.random.normal(ks[6], (E, R, D_OUT), jnp.float32) * 0.02}
    _L1_ffn_all = _L1_ffn_setup()
    _L1_ffn_in = {k: v for k, v in _L1_ffn_all.items() if k in ('base_w', 'base_b', 'router_w', 'router_b', 'lora_A', 'lora_B')}
    del _L1_ffn_all
    return {'x': x, 'itok_B_1_198': itok_B_1_198, 'itok_B_0_6': itok_B_0_6, 'L0_cond_weights': _L0_cond_in['weights'], 'L0_ffn_gate_w': _L0_ffn_in['gate_w'], 'L0_ffn_wg': _L0_ffn_in['wg'], 'L0_ffn_wu': _L0_ffn_in['wu'], 'L0_ffn_wd': _L0_ffn_in['wd'], 'L1_cond_W': _L1_cond_in['W'], 'L1_cond_A': _L1_cond_in['A'], 'L1_cond_Bm': _L1_cond_in['Bm'], 'L1_cond_scalings': _L1_cond_in['scalings'], 'L1_ffn_base_w': _L1_ffn_in['base_w'], 'L1_ffn_base_b': _L1_ffn_in['base_b'], 'L1_ffn_router_w': _L1_ffn_in['router_w'], 'L1_ffn_router_b': _L1_ffn_in['router_b'], 'L1_ffn_lora_A': _L1_ffn_in['lora_A'], 'L1_ffn_lora_B': _L1_ffn_in['lora_B']}

def reference(x, itok_B_1_198, itok_B_0_6, L0_cond_weights, L0_ffn_gate_w, L0_ffn_wg, L0_ffn_wu, L0_ffn_wd, L1_cond_W, L1_cond_A, L1_cond_Bm, L1_cond_scalings, L1_ffn_base_w, L1_ffn_base_b, L1_ffn_router_w, L1_ffn_router_b, L1_ffn_lora_A, L1_ffn_lora_B):
    import jax
    import jax.numpy as jnp

    def _L0_cond_ref(x, conditions, weights):
        import jax, jax.numpy as jnp
        import numpy as np
        B, C, T = (128, 128, 1024)
        S, D = (200, 128)
        w = weights[conditions]
        return jnp.einsum('bct,bcd->bdt', x, w)

    def _L0_ffn_ref(hidden_states, gate_w, wg, wu, wd):
        import jax, jax.numpy as jnp
        import numpy as np
        E = 64
        K = 8
        H = 1024
        I = 384
        CAP = 256

        def _moe(hidden_states, gate_w, wg, wu, wd):
            B, S, Hd = hidden_states.shape
            x = hidden_states.reshape(-1, Hd)
            T = x.shape[0]
            logits = x @ gate_w.T
            probs = jax.nn.softmax(logits.astype(jnp.float32), axis=-1)
            w, sel = jax.lax.top_k(probs, K)
            w = w / jnp.sum(w, axis=-1, keepdims=True)
            w = w.astype(x.dtype)
            eid = sel.reshape(-1)
            tok = jnp.repeat(jnp.arange(T), K)
            oh = jax.nn.one_hot(eid, E, dtype=jnp.int32)
            pos = jnp.sum(jnp.cumsum(oh, axis=0) * oh, axis=-1) - 1
            valid = pos < CAP
            slot = jnp.where(valid, pos, CAP)
            xin = jnp.zeros((E, CAP + 1, Hd), x.dtype).at[eid, slot].set(x[tok])
            inp = xin[:, :CAP]
            h = jax.nn.silu(jnp.einsum('ech,ehi->eci', inp, wg)) * jnp.einsum('ech,ehi->eci', inp, wu)
            out = jnp.einsum('eci,eih->ech', h, wd)
            out_pad = jnp.concatenate([out, jnp.zeros((E, 1, Hd), out.dtype)], axis=1)
            g = out_pad[eid, slot] * (w.reshape(-1) * valid.astype(w.dtype))[:, None]
            y = jnp.zeros((T, Hd), x.dtype).at[tok].add(g)
            return y.reshape(B, S, Hd)
        return _moe(hidden_states, gate_w, wg, wu, wd)

    def _L1_cond_ref(x, W, A, Bm, scalings, adapter_idx):
        import jax, jax.numpy as jnp
        import numpy as np
        B, T, D_IN, D_OUT = (16, 1024, 1024, 1024)
        N_ADAPTERS, RANK = (8, 16)
        H = jnp.einsum('btd,od->bto', x, W)
        A_b = A[adapter_idx]
        B_b = Bm[adapter_idx]
        s_b = scalings[adapter_idx]
        xa = jnp.einsum('btd,brd->btr', x, A_b)
        delta = jnp.einsum('btr,bor->bto', xa, B_b)
        delta = jax.lax.stop_gradient(delta * s_b[:, None, None])
        return H + delta

    def _L1_ffn_ref(x, base_w, base_b, router_w, router_b, lora_A, lora_B):
        import jax, jax.numpy as jnp
        import numpy as np
        B, S, D_IN, D_OUT, E, R = (4, 1024, 1024, 1024, 8, 16)
        SCALING = 32.0 / 16.0
        b, s, d_in = x.shape
        n = b * s
        e = lora_A.shape[0]
        d_out = lora_B.shape[-1]
        result = jnp.einsum('bsd,od->bso', x, base_w) + base_b
        logits = jnp.einsum('bsd,ed->bse', x, router_w) + router_b
        probs = jax.nn.softmax(logits.astype(jnp.float32), axis=-1)
        top_vals, top_idx = jax.lax.top_k(probs, 2)
        top_vals = top_vals / jnp.sum(top_vals, axis=-1, keepdims=True)
        top_vals = top_vals.astype(x.dtype)
        flat_idx = top_idx.reshape(n, 2)
        flat_val = top_vals.reshape(n, 2)
        gate = jnp.zeros((n, e), x.dtype).at[jnp.arange(n)[:, None], flat_idx].set(flat_val)
        xf = x.reshape(n, d_in)
        mid = jnp.einsum('nd,edr->ner', xf, lora_A)
        mid = mid * gate[:, :, None]
        lora_out = jnp.einsum('ner,erd->nd', mid, lora_B)
        return result + SCALING * lora_out.reshape(b, s, d_out)
    x = x + _L0_ffn_ref(_L0_cond_ref(x, itok_B_1_198, L0_cond_weights), L0_ffn_gate_w, L0_ffn_wg, L0_ffn_wu, L0_ffn_wd)
    x = x + _L1_ffn_ref(_L1_cond_ref(x, L1_cond_W, L1_cond_A, L1_cond_Bm, L1_cond_scalings, itok_B_0_6), L1_ffn_base_w, L1_ffn_base_b, L1_ffn_router_w, L1_ffn_router_b, L1_ffn_lora_A, L1_ffn_lora_B)
    return x

_drawn_inputs = setup_inputs


def setup_inputs(seed=0):
    import zlib

    import numpy as np

    out = dict(_drawn_inputs(seed))
    spreads = {'L1_cond_scalings': (1.0, 0.6)}
    factors = {'L1_ffn_base_b': 3.432, 'L1_ffn_router_b': 5.775}
    for name, (base, spread) in spreads.items():
        noise = np.random.default_rng([zlib.crc32(name.encode()), seed]).standard_normal(out[name].shape)
        drawn = base * np.exp(spread * noise) if base else spread * noise
        out[name] = jnp.asarray(drawn.astype(out[name].dtype))
    for name, factor in factors.items():
        out[name] = (out[name] * factor).astype(out[name].dtype)
    return out
```

```python
from contextlib import ExitStack

import concourse.bass as bass
from concourse import mybir

F32 = mybir.dt.float32
F32R = mybir.dt.float32r
BF16 = mybir.dt.bfloat16
I32 = mybir.dt.int32
ALU = mybir.AluOpType
ACT = mybir.ActivationFunctionType
AX_X = mybir.AxisListType.X

P = 128
NB = 32
D = 1024
E = 64
I = 384
CAP = 256
TOK = NB * P
ROW = D + E
NA = 8
R = 16
NX = D + NA + NA * R
CG = [(0, 384), (384, 768), (768, NX)]
UN = 1536
NRAW = 4
NHL = 8
NY = 4
ZMIN = -87.8


class Count:

    def __init__(self, eng, sem):
        self.eng, self.sem, self.n = eng, sem, 0

    def link(self, ins):
        self.n += 1
        ins.then_inc(self.sem, 1)
        self.eng.wait_ge(self.sem, self.n)


def adaln_ffn_kernel(nc, x, cond, adap, w0, gate_w, wg, wu, wd, W, A, Bm, scal,
                     base_w, base_b, router_w, router_b, lora_A, lora_B, out):
    x_r = x.rearrange("b c t -> (b c) t")
    out_r = out.rearrange("b c t -> (b c) t")
    w0_r = w0.rearrange("s c d -> (s c) d")
    yd = nc.dram_tensor("yd", (TOK + 2 * P, ROW), F32, kind="Internal").ap()
    acc = nc.dram_tensor("accd", (TOK + 2 * P, D), F32, kind="Internal").ap()
    tab = nc.dram_tensor("tabd", (E * NB + 1, P), F32, kind="Internal").ap()
    tab_v = tab[0:E * NB, :].rearrange("(e i) t -> i e t", i=NB)

    with ExitStack() as ctx:
        def sb(name, shape, dt, stack=None):
            return (stack or ctx).enter_context(nc.sbuf_tensor(name, shape, dt))

        def sem(name):
            return ctx.enter_context(nc.semaphore(name))

        ps = ctx.enter_context(nc.psum_tensor("ps", [P, 8, 512], F32))

        def bank(b, a=0, z=512, p=P):
            return ps[0:p, b, a:z]

        ident = sb("ident", [P, P], F32)
        tri = sb("tri", [P, P], BF16)
        ones = sb("ones", [P, P], BF16)
        slot = sb("slot", [P, 2], F32)
        dum = sb("dum", [P, 2], F32)
        pf = sb("pf", [P, 1], F32)
        t128 = sb("t128", [P, 2, E], F32)
        rowi = sb("rowi", [P, 2 * E], I32)
        toki = sb("toki", [P, 2 * E], I32)
        wcol = sb("wcol", [P, 2 * E], F32)
        mk = sb("mk", [P, NB], F32)
        laR = sb("laR", [P, 8, NA, R], F32)
        bmR = sb("bmR", [P, 8, NA, R], F32)

        moe = ExitStack()
        raw = sb("raw", [P, NRAW, UN], F32, moe)
        HR = sb("HR", [P, NHL, UN], F32R, moe)
        LR = sb("LR", [P, NHL, UN], F32R, moe)

        rt = ExitStack()
        wall = sb("wall", [P, NB, P], F32, rt)
        xt = sb("xt", [P, 4, D], F32, rt)
        yrow = sb("yrow", [P, NY, ROW], F32, rt)
        yT = sb("yT", [P, 2, 8, P], F32, rt)
        gT = sb("gT", [P, 8, P], F32, rt)
        gw = sb("gw", [E, D], F32, rt)
        zrow = sb("zrow", [P, ROW], F32, rt)
        e32 = sb("e32", [P, 2, E], F32, rt)
        tacc = sb("tacc", [P, 2, E], F32, rt)
        condi = sb("condi", [P, NB], I32, rt)
        adi = sb("adi", [P, NB], I32, rt)
        cidx = sb("cidx", [P, NB], I32, rt)
        scp = sb("scp", [P, 1], F32, rt)
        mkt = sb("mkt", [P, 3, NB], F32, rt)
        m8 = sb("m8", [P, 2, 8], F32, rt)
        zz = sb("zz", [P, 2, E], F32, rt)
        zr = sb("zr", [P, 2, E], F32, rt)
        eb = sb("eb", [P, 2, E], F32, rt)
        wm = sb("wm", [P, 2, E], F32, rt)
        sm = sb("sm", [P, 2, 2], F32, rt)
        mask = sb("mask", [P, 2, E], BF16, rt)
        macc = sb("macc", [P, 3, E], BF16, rt)
        ct = sb("ct", [E, 2, P], F32, rt)
        cb = sb("cb", [P, 2, E], F32, rt)
        rt.close()

        Xg = sb("Xg", [P, 2, 2, ROW], F32, moe)
        XH = sb("XH", [P, 2, 2, 8, P], F32R, moe)
        XL = sb("XL", [P, 2, 2, 8, P], F32R, moe)
        sil = sb("sil", [P, 2, I], F32, moe)
        prod = sb("prod", [P, 2, 3, P], F32, moe)
        hH = sb("hH", [P, 2, 3, P], F32R, moe)
        hL = sb("hL", [P, 2, 3, P], F32R, moe)
        ot = sb("ot", [P, 2, D], F32, moe)
        G = sb("G", [P, 2, 2, P], F32, moe)
        Gj = sb("Gj", [P, P], F32, moe)
        cnt = sb("cnt", [P, 2], F32, moe)
        moe.close()

        MH = sb("MH", [P, 9, NX], F32R)
        ML = sb("ML", [P, 9, NX], F32R)
        pre = ExitStack()
        BH = sb("BH", [P, 8, NX], F32R, pre)
        BL = sb("BL", [P, 8, NX], F32R, pre)
        bw = sb("bw", [P, 2, D], F32, pre)
        wr = sb("wr", [P, 2, 8, P], F32, pre)
        WH = sb("WH", [P, 2, 8, P], F32R, pre)
        WL = sb("WL", [P, 2, 8, P], F32R, pre)
        pre.close()
        x1 = sb("x1", [P, 6, D], F32)
        xTH = sb("xTH", [P, 2, 8, 2 * P], F32R)
        xTL = sb("xTL", [P, 2, 8, 2 * P], F32R)
        ar = sb("ar", [P, D], F32)
        ATH = sb("ATH", [P, 8, P], F32R)
        ATL = sb("ATL", [P, 8, P], F32R)
        lb = sb("lb", [P, D], F32)
        lbH = sb("lbH", [P, D], F32R)
        lbL = sb("lbL", [P, D], F32R)
        bias = sb("bias", [P, D], F32)
        rb = sb("rb", [P, NA], F32)
        xaH = sb("xaH", [P, 2, 2 * P], F32R)
        xaL = sb("xaL", [P, 2, 2 * P], F32R)
        lg2 = sb("lg2", [P, NA], F32)
        mx2 = sb("mx2", [P, 1], F32)
        z2 = sb("z2", [P, 14], F32)
        t8 = sb("t8", [P, 8], F32)
        zr2 = sb("zr2", [P, 14], F32)
        e2 = sb("e2", [P, 2, NA], F32)
        g2 = sb("g2", [P, NA], F32)
        sm2 = sb("sm2", [P, 2], F32)
        gate = sb("gate", [P, NA], F32)
        mg = sb("mg", [P, P], F32)
        mgH = sb("mgH", [P, P], F32R)
        mgL = sb("mgL", [P, P], F32R)
        osb = sb("osb", [P, 3, D], F32)

        d_small, d_bc, d_gw, d_la = sem("d_small"), sem("d_bc"), sem("d_gw"), sem("d_la")
        d_z = sem("d_z")
        d_x = [sem(f"d_x{i}") for i in range(4)]
        d_as = [sem(f"d_as{i}") for i in range(4)]
        d_ys = [sem(f"d_ys{i}") for i in range(NY)]
        d_ts = [sem(f"d_ts{i}") for i in range(2)]
        d_w = [sem(f"d_w{i}") for i in range(4)]
        s_pc, s_cst, s_cidx, s_dv, s_zr = sem("s_pc"), sem("s_cst"), sem("s_cidx"), sem("s_dv"), sem("s_zr")
        s_gt, s_gte = sem("s_gt"), sem("s_gte")
        s_Y, s_yr, s_T, s_yT, s_lg = sem("s_Y"), sem("s_yr"), sem("s_T"), sem("s_yT"), sem("s_lg")
        s_z, s_e, s_rt, s_wy, s_mask, s_cum = sem("s_z"), sem("s_e"), sem("s_rt"), sem("s_wy"), sem("s_mask"), sem("s_cum")
        s_cte, s_cb, s_idx = sem("s_cte"), sem("s_cb"), sem("s_idx")
        d_raw = [sem(f"d_raw{i}") for i in range(NRAW)]
        s_H, s_L, s_k, s_dn = sem("s_H"), sem("s_L"), sem("s_k"), sem("s_dn")
        s_f, s_fh, s_fl = sem("s_f"), sem("s_fh"), sem("s_fl")
        s_sl, s_hp, s_out, s_tok, s_wc = sem("s_sl"), sem("s_hp"), sem("s_out"), sem("s_tok"), sem("s_wc")
        d_g = [sem(f"d_g{i}") for i in range(2)]
        d_xg = [sem(f"d_xg{i}") for i in range(2)]
        d_sc = sem("d_sc")
        d_bw = [sem(f"d_bw{i}") for i in range(2)]
        d_wr = [sem(f"d_wr{i}") for i in range(2)]
        s_bf, s_bh, s_bl, s_wh, s_wl = sem("s_bf"), sem("s_bh"), sem("s_bl"), sem("s_wh"), sem("s_wl")
        s_m, s_mh, s_ml = sem("s_m"), sem("s_mh"), sem("s_ml")
        d_ab, d_bi = sem("d_ab"), sem("d_bi")
        d_x1 = [sem(f"d_x1{i}") for i in range(6)]
        d_o = [sem(f"d_o{i}") for i in range(3)]
        s_at, s_ath, s_atl, s_lbh, s_lbl = sem("s_at"), sem("s_ath"), sem("s_atl"), sem("s_lbh"), sem("s_lbl")
        s_xf, s_xh, s_xl = sem("s_xf"), sem("s_xh"), sem("s_xl")
        s_xa, s_xah, s_xal = sem("s_xa"), sem("s_xah"), sem("s_xal")
        s_mm, s_z2, s_e2, s_mg, s_mt, s_mth, s_mtl = [sem(n) for n in ("s_mm", "s_z2", "s_e2", "s_mg", "s_mt", "s_mth", "s_mtl")]
        s_lo, s_fin, s_pb, s_pad = sem("s_lo"), sem("s_fin"), sem("s_pb"), sem("s_pad")

        units, pos = [], {}

        def stream(kinds, e):
            for k in kinds:
                pos[(k, e)] = len(units)
                units.append((k, e))

        stream(["gA", "uA", "gB", "uB"], 0)
        for e in range(1, E):
            stream(["gA", "uA", "gB", "uB"], e)
            stream(["dA", "dB"], e - 1)
        stream(["dA", "dB"], E - 1)

        def unit_src(n):
            k, e = units[n]
            h = 0 if k[1] == "A" else UN
            if k[0] == "d":
                v = wd[e].rearrange("(p j) h -> p (j h)", j=3)
            else:
                v = (wg if k[0] == "g" else wu)[e].rearrange("(p k) i -> p (k i)", k=8)
            return v[:, h:h + UN]

        def wait_retired(eng, n):
            k, e = units[n]
            if k[0] == "d":
                eng.wait_ge(s_dn, 4 * (e + 1))
            else:
                eng.wait_ge(s_k, 2 * e + (1 if k[1] == "A" else 2))

        fq = {}
        for j in range(4):
            fq[("x", 0, j)] = len(fq)
        for e in range(E):
            if e + 1 < E:
                for j in range(4):
                    fq[("x", e + 1, j)] = len(fq)
            for c in range(2):
                fq[("h", e, c)] = len(fq)

        def bcast(ap1, n):
            return ap1.rearrange("(a n) -> a n", a=1).to_broadcast([P, n])

        block = ctx.enter_context(nc.Block())

        @block.sync
        def _(eng):
            eng.dma_start(condi[:, :], bcast(cond, NB)).then_inc(d_small, 16)
            eng.dma_start(gw[:, :], gate_w).then_inc(d_gw, 16)
            eng.dma_start(adi[:, :], bcast(adap, NB)).then_inc(d_bc, 16)
            for a in range(NA):
                eng.dma_start(scp[R * a:R * a + R, :],
                              scal[a:a + 1].rearrange("(a n) -> a n", a=1).to_broadcast([R, 1])).then_inc(d_bc, 16)

            def load_unit(n):
                if n >= NRAW:
                    eng.wait_ge(s_L, n - NRAW + 1)
                eng.dma_start(raw[:, n % NRAW, :], unit_src(n)).then_inc(d_raw[n % NRAW], 16)

            def store_y(i):
                eng.wait_ge(s_yr, 2 * i + 2)
                eng.wait_ge(s_wy, i + 1)
                eng.dma_start(yd[i * P:(i + 1) * P, :], yrow[:, i % NY, :]).then_inc(d_ys[i % NY], 16)

            def store_t(i):
                eng.wait_ge(s_cte, i + 1)
                eng.dma_start(tab_v[i], ct[:, i % 2, :]).then_inc(d_ts[i % 2], 16)

            for i in range(NB + 4):
                if i < NB:
                    if i >= 4:
                        eng.wait_ge(s_Y, 2 * (i - 3))
                        eng.wait_ge(d_as[i % 4], 16 * (i // 4))
                    eng.dma_start(xt[:, i % 4, :], x_r[i * P:(i + 1) * P, :]).then_inc(d_x[i % 4], 16)
                if i == 3:
                    eng.wait_ge(s_zr, 1)
                    for c in range(2):
                        r0 = TOK + c * P
                        eng.dma_start(yd[r0:r0 + P, :], zrow[:, :]).then_inc(d_z, 16)
                        eng.dma_start(acc[r0:r0 + P, :], zrow[:, 0:D]).then_inc(d_z, 16)
                    eng.dma_start(tab[E * NB:E * NB + 1, :], zrow[0:1, 0:P]).then_inc(d_z, 16)
                if 1 <= i <= NB:
                    j = i - 1
                    eng.wait_ge(d_x[j % 4], 16 * (j // 4 + 1))
                    eng.dma_start(acc[j * P:(j + 1) * P, :], xt[:, j % 4, :]).then_inc(d_as[j % 4], 16)
                if i >= 3 and i - 3 < NB:
                    store_y(i - 3)
                if i >= 4:
                    store_t(i - 4)
                if i == 22:
                    for n in range(NRAW):
                        load_unit(n)
                if i == 12:
                    for e in range(NA):
                        with nc.allow_non_contiguous_dma(reason="64-byte rows"):
                            eng.dma_start(laR[:, :, e, :],
                                          lora_A[e].rearrange("(q p) r -> p q r", p=P)).then_inc(d_la, 16)
                            eng.dma_start(bmR[:, :, e, :],
                                          Bm[e].rearrange("(q p) r -> p q r", p=P)).then_inc(d_la, 16)
            for n in range(NRAW, len(units)):
                load_unit(n)

            eng.wait_ge(s_dn, 4 * E)
            eng.wait_ge(s_out, 4 * E)
            eng.wait_ge(d_sc, 32 * E)
            eng.dma_start(bw[0:NA, 0, :], router_w).then_inc(d_bw[0], 16)
            for k in range(2):
                eng.dma_start(wr[:, k, :, :], W.rearrange("(q p) d -> p q d", p=P)[:, :, k * P:(k + 1) * P])\
                   .then_inc(d_wr[k], 16)
            for j in range(8):
                s = (j + 1) % 2
                if j >= 1:
                    eng.wait_ge(s_bf, 1 + 2 * (j - 1))
                eng.dma_start(bw[:, s, :], base_w[j * P:(j + 1) * P, :]).then_inc(d_bw[s], 16)
            for k in range(2, 8):
                eng.wait_ge(s_wl, k - 1)
                eng.dma_start(wr[:, k % 2, :, :], W.rearrange("(q p) d -> p q d", p=P)[:, :, k * P:(k + 1) * P])\
                   .then_inc(d_wr[k % 2], 16)
            eng.wait_ge(s_m, 9)
            eng.dma_start(ar[:, :], A.rearrange("a r d -> (a r) d")).then_inc(d_ab, 16)
            for t in range(4):
                eng.dma_start(x1[:, t, :], acc[t * P:(t + 1) * P, :]).then_inc(d_x1[t], 16)
            eng.dma_start(bias[:, :], bcast(base_b, D)).then_inc(d_bi, 16)
            eng.dma_start(rb[:, :], bcast(router_b, NA)).then_inc(d_bi, 16)
            eng.dma_start(lb[:, :], lora_B.rearrange("e r d -> (e r) d")).then_inc(d_ab, 16)
            for t in range(4, NB + 6):
                if t >= 6:
                    eng.wait_ge(s_fin, 2 * (t - 5))
                    eng.dma_start(out_r[(t - 6) * P:(t - 5) * P, :], osb[:, t % 3, :]).then_inc(d_o[t % 3], 16)
                if t < NB:
                    eng.dma_start(x1[:, t % 6, :], acc[t * P:(t + 1) * P, :]).then_inc(d_x1[t % 6], 16)
            for s in range(3):
                eng.wait_ge(d_o[s], 16 * len(range(s, NB, 3)))

        @block.gpsimd
        def _(eng):
            ch = Count(eng, s_pc)
            eng.memset(ident[:, :], 0.0)
            eng.memset(ones[:, :], 1.0)
            ch.link(eng.memset(tri[:, :], 1.0))
            eng.affine_select(out=ident[:, :], in_=ident[:, :], compare_op=ALU.not_equal, fill=1.0,
                              base=0, pattern=[[-1, P]], channel_multiplier=1)
            eng.affine_select(out=tri[:, :], in_=tri[:, :], compare_op=ALU.is_ge, fill=0.0,
                              base=0, pattern=[[1, P]], channel_multiplier=-1)
            eng.iota(pf[:, :], [[0, 1]], base=0, channel_multiplier=1, allow_small_or_imprecise_dtypes=True)
            eng.iota(slot[:, :], [[P, 2]], base=0, channel_multiplier=1, allow_small_or_imprecise_dtypes=True)
            eng.iota(dum[:, :], [[P, 2]], base=TOK, channel_multiplier=1, allow_small_or_imprecise_dtypes=True)
            eng.iota(e32[:, :, :], [[0, 2], [NB, E]], base=0, channel_multiplier=0,
                     allow_small_or_imprecise_dtypes=True).then_inc(s_cst, 1)
            eng.wait_ge(s_cidx, 1)
            for b in range(NB):
                eng.indirect_dma_start(wall[:, b, :], None, w0_r,
                                       bass.IndirectOffsetOnAxis(ap=cidx[:, b:b + 1], axis=0))\
                   .then_inc(d_w[b // 8], 16)

            def gather_tab(e):
                if e == 0:
                    for s in range(2):
                        eng.wait_ge(d_ts[s], 16 * (NB // 2))
                    for s in range(NY):
                        eng.wait_ge(d_ys[s], 16 * len(range(s, NB, NY)))
                    for s in range(4):
                        eng.wait_ge(d_as[s], 16 * (NB // 4))
                    eng.wait_ge(d_z, 80)
                    eng.wait_ge(s_idx, 1)
                if e >= 2:
                    eng.wait_ge(s_tok, 2 * (e - 1))
                for c in range(2):
                    eng.indirect_dma_start(G[:, e % 2, c, :], None, tab,
                                           bass.IndirectOffsetOnAxis(ap=rowi[:, c * E + e:c * E + e + 1], axis=0))\
                       .then_inc(d_g[e % 2], 16)

            def gather_x(e):
                eng.wait_ge(s_tok, 2 * (e + 1))
                if e >= 2:
                    eng.wait_ge(s_f, fq[("x", e - 2, 3)] + 1)
                    eng.wait_ge(s_wc, e - 1)
                for c in range(2):
                    eng.indirect_dma_start(Xg[:, e % 2, c, :], None, yd,
                                           bass.IndirectOffsetOnAxis(ap=toki[:, c * E + e:c * E + e + 1], axis=0))\
                       .then_inc(d_xg[e % 2], 16)

            def scatter(e):
                if e >= 1:
                    eng.wait_ge(d_sc, 32 * e)
                for c in range(2):
                    eng.wait_ge(s_out, 4 * e + 2 * c + 2)
                    eng.indirect_dma_start(acc, bass.IndirectOffsetOnAxis(ap=toki[:, c * E + e:c * E + e + 1], axis=0),
                                           ot[:, c, :], None, compute_op=ALU.add).then_inc(d_sc, 16)

            gather_tab(0)
            gather_tab(1)
            gather_x(0)
            gather_tab(2)
            gather_x(1)
            for e in range(E + 1):
                if e + 2 < E:
                    gather_x(e + 2)
                if e + 3 < E:
                    gather_tab(e + 3)
                if e >= 1:
                    scatter(e - 1)
            eng.wait_ge(d_sc, 32 * E)

            eng.wait_ge(d_bi, 32)
            for t in range(NB):
                eng.wait_ge(d_x1[t % 6], 16 * (t // 6 + 1))
                eng.wait_ge(s_xf, 2 * (t + 1))
                eng.tensor_tensor(x1[:, t % 6, :], x1[:, t % 6, :], bias[:, :], ALU.add).then_inc(s_pb, 1)

        @block.tensor
        def _(eng):
            eng.wait_ge(s_cst, 1)
            eng.wait_ge(d_gw, 16)
            for k in range(8):
                mm = eng.transpose(bank(4, k * E, (k + 1) * E), gw[:, k:D:8], ident[0:E, 0:E])
            mm.then_inc(s_gt, 1)

            def condition(i):
                eng.wait_ge(d_w[i // 8], 16 * 8)
                eng.wait_ge(d_x[i % 4], 16 * (i // 4 + 1))
                for h in range(2):
                    if i:
                        eng.wait_ge(s_yr, 2 * i - 1 + h)
                    eng.matmul(bank(h), wall[:, i, :], xt[:, i % 4, h * 512:(h + 1) * 512],
                               start=True, stop=True).then_inc(s_Y, 1)

            def turn(i):
                eng.wait_ge(s_yr, 2 * i + 2)
                for f in range(2):
                    n = 2 * i + f
                    if n >= 2:
                        eng.wait_ge(s_yT, n - 1)
                    for q in range(4):
                        k = 4 * f + q
                        mm = eng.transpose(bank(2 + f, q * P, (q + 1) * P), yrow[:, i % NY, k * P:(k + 1) * P],
                                           ident[:, :])
                    mm.then_inc(s_T, 1)

            def logits(i):
                if i == 0:
                    eng.wait_ge(s_gte, 1)
                eng.wait_ge(s_yT, 2 * i + 2)
                if i >= 2:
                    eng.wait_ge(s_rt, i - 1)
                for k in range(8):
                    mm = eng.matmul(bank(4 + i % 2, 0, P), yT[:, i % 2, k, :], gT[:, k, :], start=(k == 0), stop=(k == 7))
                mm.then_inc(s_lg, 1)

            def counts(i):
                eng.wait_ge(s_mask, 2 * i + 2)
                if i >= 2:
                    eng.wait_ge(s_cte, i - 1)
                b = 6 + i % 2
                eng.matmul(bank(b, 0, P, E), mask[:, i % 2, :], tri[:, :], start=True, stop=(i == 0))
                if i:
                    eng.matmul(bank(b, 0, P, E), macc[:, (i - 1) % 3, :], ones[:, :], start=False, stop=True)
                eng.matmul(bank(b, P, P + E), ones[:, :], macc[:, i % 3, :], start=True, stop=True)\
                   .then_inc(s_cum, 1)

            for i in range(NB + 4):
                if i < NB:
                    condition(i)
                if 1 <= i <= NB:
                    turn(i - 1)
                if 2 <= i <= NB + 1:
                    logits(i - 2)
                if i >= 4:
                    counts(i - 4)

            def turn_x(e, j):
                q = fq[("x", e, j)]
                c, h = divmod(j, 2)
                if j == 0:
                    eng.wait_ge(d_xg[e % 2], 32 * (e // 2 + 1))
                if q >= 2:
                    eng.wait_ge(s_fl, q - 1)
                else:
                    eng.wait_ge(s_rt, NB)
                    eng.wait_ge(s_cte, NB)
                for r in range(4):
                    k = 4 * h + r
                    mm = eng.transpose(bank(6 + q % 2, r * P, (r + 1) * P), Xg[:, e % 2, c, k * P:(k + 1) * P],
                                       ident[:, :])
                mm.then_inc(s_f, 1)

            def turn_h(e, c):
                q = fq[("h", e, c)]
                eng.wait_ge(s_fl, q - 1)
                eng.wait_ge(s_hp, 2 * e + c + 1)
                for j in range(3):
                    mm = eng.transpose(bank(6 + q % 2, j * P, (j + 1) * P), prod[:, c, j, :], ident[:, :])
                mm.then_inc(s_f, 1)

            def up(e):
                eng.wait_ge(s_fl, fq[("x", e, 3)] + 1)
                if e >= 1:
                    eng.wait_ge(s_hp, 2 * e)
                for k in range(8):
                    half = "A" if k < 4 else "B"
                    n = pos[("u" + half, e)]
                    if k % 4 == 0:
                        eng.wait_ge(s_L, n + 1)
                    o = (k % 4) * I
                    gs, us = (n - 1) % NHL, n % NHL
                    for c in range(2):
                        ops = [(XH, HR, gs, 0), (XH, HR, us, 1), (XH, LR, gs, 0), (XH, LR, us, 1),
                               (XL, HR, gs, 0), (XL, HR, us, 1)]
                        for m, (X, Wt, s, g) in enumerate(ops):
                            mm = eng.matmul(bank(2 * c + g, 0, I), X[:, e % 2, c, k, :], Wt[:, s, o:o + I],
                                            start=(k == 0 and m < 2), stop=(k == 7 and m >= 4))
                    if k in (3, 7):
                        mm.then_inc(s_k, 1)
                    if k % 2 == 1 and e + 1 < E:
                        turn_x(e + 1, k // 2)

            def down(e):
                eng.wait_ge(s_fl, fq[("h", e, 1)] + 1)
                eng.wait_ge(s_L, pos[("dB", e)] + 1)
                for c in range(2):
                    for h in range(2):
                        o = 4 * e + 2 * c + h
                        if o >= 2:
                            eng.wait_ge(s_out, o - 1)
                        for j in range(3):
                            flat = j * D + h * 512
                            s = (pos[("dA", e)] + flat // UN) % NHL
                            f = flat % UN
                            for m, (X, Wt) in enumerate([(hH, HR), (hL, HR), (hH, LR)]):
                                mm = eng.matmul(bank(4 + h), X[:, c, j, :], Wt[:, s, f:f + 512],
                                                start=(j == 0 and m == 0), stop=(j == 2 and m == 2))
                        mm.then_inc(s_dn, 1)

            for j in range(4):
                turn_x(0, j)
            for e in range(E):
                up(e)
                if e >= 1:
                    down(e - 1)
                for c in range(2):
                    turn_h(e, c)
            down(E - 1)

            eng.wait_ge(s_out, 4 * E)
            eng.wait_ge(s_hp, 2 * E)
            eng.wait_ge(s_fl, len(fq))
            eng.wait_ge(d_bw[0], 16)
            for q in range(8):
                mm = eng.transpose(bank(6, q * NA, (q + 1) * NA), bw[0:NA, 0, q * P:(q + 1) * P], ident[0:NA, 0:NA])
            mm.then_inc(s_bf, 1)
            for j in range(8):
                s = (j + 1) % 2
                eng.wait_ge(d_bw[s], 16 * (1 + (j + 1) // 2 if s == 0 else j // 2 + 1))
                for f in range(2):
                    n = 1 + 2 * j + f
                    if n >= 2:
                        eng.wait_ge(s_bl, n)
                    for r in range(4):
                        q = 4 * f + r
                        mm = eng.transpose(bank(6 + n % 2, r * P, (r + 1) * P), bw[:, s, q * P:(q + 1) * P], ident[:, :])
                    mm.then_inc(s_bf, 1)
            eng.wait_ge(s_bl, 18)
            for k in range(9):
                eng.wait_ge(s_wl, k + 1)
                if k >= 2:
                    eng.wait_ge(s_ml, k - 1)
                b0 = 3 * (k % 2)
                for q in range(8):
                    for m, (X, Y) in enumerate([(WH, BH), (WH, BL), (WL, BH)]):
                        for g, (a, z) in enumerate(CG):
                            mm = eng.matmul(bank(b0 + g, 0, z - a), X[:, k % 2, q, :], Y[:, q, a:z],
                                            start=(q == 0 and m == 0), stop=(q == 7 and m == 2))
                mm.then_inc(s_m, 1)

            eng.wait_ge(d_ab, 32)
            for f in range(2):
                for r in range(4):
                    k = 4 * f + r
                    mm = eng.transpose(bank(6 + f, r * P, (r + 1) * P), ar[:, k * P:(k + 1) * P], ident[:, :])
                mm.then_inc(s_at, 1)

            def turn_t(t, f):
                n = 2 * t + f
                if f == 0:
                    eng.wait_ge(d_x1[t % 6], 16 * (t // 6 + 1))
                if n:
                    eng.wait_ge(s_xl, n)
                else:
                    eng.wait_ge(s_atl, 2)
                for r in range(4):
                    k = 4 * f + r
                    mm = eng.transpose(bank(6, r * P, (r + 1) * P), x1[:, t % 6, k * P:(k + 1) * P], ident[:, :])
                mm.then_inc(s_xf, 1)

            def adapter(g):
                eng.wait_ge(s_xl, 4 * (g + 1))
                if g:
                    eng.wait_ge(s_xal, 2 * g)
                    eng.wait_ge(s_mtl, 2 * g - 1)
                for k in range(8):
                    for m, (X, Y) in enumerate([(ATH, xTH), (ATH, xTL), (ATL, xTH)]):
                        mm = eng.matmul(bank(7, 0, 256), X[:, k, :], Y[:, g % 2, k, :],
                                        start=(k == 0 and m == 0), stop=(k == 7 and m == 2))
                mm.then_inc(s_xa, 1)

            def turn_m(t):
                eng.wait_ge(s_mg, t + 1)
                eng.wait_ge(s_xal, 2 * min((t + 1) // 2 + 1, NB // 2))
                if t:
                    eng.wait_ge(s_mtl, t)
                eng.transpose(bank(7, 256, 384), mg[:, :], ident[:, :]).then_inc(s_mt, 1)

            def lora(t):
                eng.wait_ge(s_mtl, t + 1)
                b0 = 3 * (t % 2)
                for m, (X, Y) in enumerate([(mgH, lbH), (mgH, lbL), (mgL, lbH)]):
                    for g, (a, z) in enumerate(CG):
                        z = min(z, D)
                        mm = eng.matmul(bank(b0 + g, 0, z - a), X[:, :], Y[:, a:z], start=False, stop=(m == 2),
                                        skip_group_check=True)
                mm.then_inc(s_lo, 1)

            for t in range(2):
                for f in range(2):
                    turn_t(t, f)
            adapter(0)
            for t in range(NB):
                g, o = t // 2, (t % 2) * P
                if t >= 2:
                    eng.wait_ge(s_fin, 2 * (t - 1))
                else:
                    eng.wait_ge(s_ml, 9)
                if t == 0:
                    eng.wait_ge(s_lbl, 1)
                b0 = 3 * (t % 2)
                for k in range(9):
                    if k == 8:
                        eng.wait_ge(s_xal, 2 * (g + 1))
                        ops = [(xaH[:, g % 2, o:o + P], MH), (xaH[:, g % 2, o:o + P], ML), (xaL[:, g % 2, o:o + P], MH)]
                    else:
                        xh, xl = xTH[:, g % 2, k, o:o + P], xTL[:, g % 2, k, o:o + P]
                        ops = [(xh, MH), (xh, ML), (xl, MH)]
                    for m, (X, Y) in enumerate(ops):
                        for n, (a, z) in enumerate(CG):
                            mm = eng.matmul(bank(b0 + n, 0, z - a), X, Y[:, k, a:z],
                                            start=(k == 0 and m == 0), stop=(k == 8 and m == 2))
                    if k == 8:
                        mm.then_inc(s_mm, 1)
                    if k in (2, 5) and t + 2 < NB:
                        turn_t(t + 2, (k - 2) // 3)
                    if k == 3 and t:
                        turn_m(t - 1)
                    if k == 6 and t:
                        lora(t - 1)
                if t % 2 and t + 1 < NB:
                    adapter(g + 1)
            turn_m(NB - 1)
            lora(NB - 1)

        @block.scalar
        def _(eng):
            def evac_y(i):
                if i >= NY:
                    eng.wait_ge(d_ys[i % NY], 16 * (i // NY))
                    eng.wait_ge(s_T, 2 * (i - NY) + 2)
                for h in range(2):
                    eng.wait_ge(s_Y, 2 * i + h + 1)
                    eng.activation(yrow[:, i % NY, 0:D].rearrange("q (k p) -> q p k", k=8)[:, 64 * h:64 * h + 64, :],
                                   bank(h).rearrange("q (p k) -> q p k", k=8), ACT.Copy).then_inc(s_yr, 1)

            def exps(i):
                eng.wait_ge(s_z, i + 1)
                if i >= 2:
                    eng.wait_ge(s_wy, i - 1)
                eng.activation(eb[:, i % 2, :], zz[:, i % 2, :], ACT.Exp).then_inc(s_e, 1)

            def evac_c(i):
                eng.wait_ge(s_cum, i + 1)
                if i >= 2:
                    eng.wait_ge(d_ts[i % 2], 16 * (i // 2))
                    eng.wait_ge(s_cb, i - 1)
                eng.activation(ct[:, i % 2, :], bank(6 + i % 2, 0, P, E), ACT.Copy)
                eng.activation(cb[:, i % 2, :], bank(6 + i % 2, P, P + E), ACT.Copy).then_inc(s_cte, 1)

            for i in range(NB + 4):
                if i < NB:
                    evac_y(i)
                if 3 <= i <= NB + 2:
                    exps(i - 3)
                if i >= 4:
                    evac_c(i - 4)

            def split(k, e):
                n = pos[(k, e)]
                eng.wait_ge(d_raw[n % NRAW], 16 * (n // NRAW + 1))
                if n >= NHL:
                    wait_retired(eng, n - NHL)
                eng.activation(HR[:, n % NHL, :], raw[:, n % NRAW, :], ACT.Copy).then_inc(s_H, 1)

            def high_x(e, j):
                q = fq[("x", e, j)]
                c, h = divmod(j, 2)
                eng.wait_ge(s_f, q + 1)
                eng.activation(XH[:, e % 2, c, 4 * h:4 * h + 4, :], bank(6 + q % 2), ACT.Copy).then_inc(s_fh, 1)

            def high_h(e, c):
                q = fq[("h", e, c)]
                eng.wait_ge(s_f, q + 1)
                eng.activation(hH[:, c, :, :], bank(6 + q % 2, 0, I), ACT.Copy).then_inc(s_fh, 1)

            def silu(e, c):
                eng.wait_ge(s_k, 2 * e + 2)
                if e:
                    eng.wait_ge(s_hp, 2 * (e - 1) + c + 1)
                eng.activation(sil[:, c, :], bank(2 * c, 0, I), ACT.Silu).then_inc(s_sl, 1)

            def result(e, c, h):
                if e:
                    eng.wait_ge(d_sc, 32 * e)
                eng.wait_ge(s_wc, e + 1)
                eng.wait_ge(s_dn, 4 * e + 2 * c + h + 1)
                eng.activation(ot[:, c, h * 512:(h + 1) * 512], bank(4 + h), ACT.Copy,
                               scale=wcol[:, c * E + e:c * E + e + 1]).then_inc(s_out, 1)

            for k in ("gA", "uA", "gB", "uB"):
                split(k, 0)
            for j in range(4):
                high_x(0, j)
            for e in range(E + 1):
                if e >= 1:
                    high_h(e - 1, 0)
                    high_h(e - 1, 1)
                if e + 1 < E:
                    split("gA", e + 1)
                    split("uA", e + 1)
                    high_x(e + 1, 0)
                    high_x(e + 1, 1)
                    split("gB", e + 1)
                    split("uB", e + 1)
                    high_x(e + 1, 2)
                    high_x(e + 1, 3)
                if e < E:
                    silu(e, 0)
                    silu(e, 1)
                    split("dA", e)
                if e >= 1:
                    result(e - 1, 0, 0)
                    result(e - 1, 0, 1)
                if e < E:
                    split("dB", e)
                if e >= 1:
                    result(e - 1, 1, 0)
                    result(e - 1, 1, 1)

            eng.wait_ge(s_dn, 4 * E)
            eng.wait_ge(d_sc, 32 * E)
            eng.wait_ge(d_la, 16 * 16)
            eng.activation(BH[:, :, D + NA:NX], laR[:, :, :, :].rearrange("p q a r -> p q (a r)"), ACT.Copy)\
               .then_inc(s_bh, 1)
            for n in range(17):
                eng.wait_ge(s_bf, n + 1)
                if n == 0:
                    eng.activation(BH[:, :, D:D + NA], bank(6, 0, 64).rearrange("p (q a) -> p q a", q=8), ACT.Copy)\
                       .then_inc(s_bh, 1)
                else:
                    j, f = divmod(n - 1, 2)
                    eng.activation(BH[:, 4 * f:4 * f + 4, j * P:(j + 1) * P],
                                   bank(6 + n % 2).rearrange("p (q n) -> p q n", q=4), ACT.Copy).then_inc(s_bh, 1)

            def high_w(k):
                if k < 8:
                    eng.wait_ge(d_wr[k % 2], 16 * (k // 2 + 1))
                    src = wr[:, k % 2, :, :]
                else:
                    src = bmR[:, :, :, :].rearrange("p q a r -> p q (a r)")
                if k >= 2:
                    eng.wait_ge(s_m, k - 1)
                eng.activation(WH[:, k % 2, :, :], src, ACT.Copy).then_inc(s_wh, 1)

            def high_m(k):
                eng.wait_ge(s_m, k + 1)
                b0 = 3 * (k % 2)
                eng.activation(MH[:, k, 0:768].rearrange("p (g n) -> p g n", g=2), ps[:, b0:b0 + 2, 0:384], ACT.Copy)
                eng.activation(MH[:, k, 768:NX], bank(b0 + 2, 0, NX - 768), ACT.Copy).then_inc(s_mh, 1)

            high_w(0)
            high_w(1)
            for k in range(9):
                high_m(k)
                if k + 2 < 9:
                    high_w(k + 2)

            eng.wait_ge(d_ab, 32)
            eng.activation(lbH[:, :], lb[:, :], ACT.Copy).then_inc(s_lbh, 1)
            for f in range(2):
                eng.wait_ge(s_at, f + 1)
                eng.activation(ATH[:, 4 * f:4 * f + 4, :], bank(6 + f), ACT.Copy).then_inc(s_ath, 1)

            def high_t(t, f):
                eng.wait_ge(s_xf, 2 * t + f + 1)
                g, o = t // 2, (t % 2) * P
                eng.activation(xTH[:, g % 2, 4 * f:4 * f + 4, o:o + P], bank(6).rearrange("p (k n) -> p k n", k=4),
                               ACT.Copy).then_inc(s_xh, 1)

            def high_a(g):
                eng.wait_ge(s_xa, g + 1)
                for o in range(2):
                    b = 2 * g + o
                    eng.activation(xaH[:, g % 2, o * P:(o + 1) * P], bank(7, o * P, (o + 1) * P), ACT.Copy,
                                   scale=mk[:, b:b + 1]).then_inc(s_xah, 1)

            def exp2(t):
                eng.wait_ge(s_z2, t + 1)
                if t >= 2:
                    eng.wait_ge(s_mg, t - 1)
                eng.activation(e2[:, t % 2, :], z2[:, 0:NA], ACT.Exp).then_inc(s_e2, 1)

            def high_g(t):
                eng.wait_ge(s_mt, t + 1)
                if t:
                    eng.wait_ge(s_lo, t)
                eng.activation(mgH[:, :], bank(7, 256, 384), ACT.Copy).then_inc(s_mth, 1)

            for t in range(2):
                for f in range(2):
                    high_t(t, f)
            high_a(0)
            for t in range(NB):
                if t:
                    exp2(t - 1)
                if t + 2 < NB:
                    high_t(t + 2, 0)
                if t:
                    high_g(t - 1)
                if t + 2 < NB:
                    high_t(t + 2, 1)
                if t % 2 and t + 1 < NB:
                    high_a(t // 2 + 1)
            exp2(NB - 1)
            high_g(NB - 1)

        @block.vector
        def _(eng):
            ch = Count(eng, s_dv)
            eng.memset(zrow[:, :], 0.0).then_inc(s_zr, 1)
            eng.memset(gT[:, :, :], 0.0)
            eng.memset(tacc[:, :, :], 0.0)
            ch.link(eng.memset(sm[:, :, :], 0.0))
            eng.wait_ge(d_small, 16)
            eng.wait_ge(s_cst, 1)
            eng.tensor_scalar(cidx[:, :], condi[:, :], float(P), pf[:, 0:1], ALU.mult, ALU.add).then_inc(s_cidx, 1)
            eng.wait_ge(s_gt, 1)
            eng.tensor_copy(gT[:, :, 0:E], bank(4).rearrange("p (k e) -> p k e", k=8)).then_inc(s_gte, 1)
            eng.wait_ge(d_bc, 16 * 9)
            ch.link(eng.tensor_scalar(mkt[:, 0, :], adi[:, :], -float(R), pf[:, 0:1], ALU.mult, ALU.add))
            ch.link(eng.tensor_scalar(mkt[:, 1, :], mkt[:, 0, :], 0.0, scp[:, 0:1], ALU.is_ge, ALU.mult))
            eng.scalar_tensor_tensor(mk[:, :], mkt[:, 0, :], R - 0.5, mkt[:, 1, :], ALU.is_le, ALU.mult)

            def evac_t(i, f):
                eng.wait_ge(s_T, 2 * i + f + 1)
                if i >= 2:
                    eng.wait_ge(s_lg, i - 1)
                eng.tensor_copy(yT[:, i % 2, 4 * f:4 * f + 4, :], bank(2 + f)).then_inc(s_yT, 1)

            def route(i):
                b = i % 2
                lg = bank(4 + b, 0, E)
                eng.wait_ge(s_lg, i + 1)
                ch.link(eng.max(m8[:, 0, :], lg))
                eng.tensor_scalar(m8[:, 1, :], m8[:, 0, :], m8[:, 0, 0:1], ZMIN, ALU.subtract, ALU.max)
                eng.tensor_scalar(zz[:, b, :], lg, m8[:, 0, 0:1], ZMIN, ALU.subtract, ALU.max).then_inc(s_z, 1)
                ch.link(eng.tensor_copy(sm[:, 1, 0:1], m8[:, 0, 0:1]))
                ch.link(eng.match_replace(zr[:, b, :], m8[:, 1, :], zz[:, b, :], 1.0))
                if i >= 2:
                    eng.wait_ge(s_cum, i - 1)
                eng.tensor_scalar(mask[:, b, :], zr[:, b, :], 0.5, None, ALU.is_ge).then_inc(s_mask, 1)
                if i:
                    eng.scalar_tensor_tensor(macc[:, i % 3, :], zr[:, b, :], 0.5, macc[:, (i - 1) % 3, :],
                                             ALU.is_ge, ALU.add).then_inc(s_mask, 1)
                else:
                    eng.tensor_scalar(macc[:, 0, :], zr[:, b, :], 0.5, None, ALU.is_ge).then_inc(s_mask, 1)

            def weigh(i):
                b = i % 2
                eng.wait_ge(s_e, i + 1)
                ch.link(eng.scalar_tensor_tensor(wm[:, b, :], zr[:, b, :], 0.5, eb[:, b, :], ALU.is_ge, ALU.mult,
                                                 accum_out=sm[:, 0, 0:1]))
                ch.link(eng.reciprocal(sm[:, 0, 1:2], sm[:, 0, 0:1]))
                eng.tensor_scalar(yrow[:, i % NY, D:ROW], wm[:, b, :], sm[:, 0, 1:2], None, ALU.mult).then_inc(s_wy, 1)

            def tiles(i):
                eng.wait_ge(s_cte, i + 1)
                eng.scalar_tensor_tensor(tacc[:, 0, :], cb[:, i % 2, :], slot[:, 0:1], tacc[:, 0, :],
                                         ALU.is_le, ALU.add)
                ch.link(eng.scalar_tensor_tensor(tacc[:, 1, :], cb[:, i % 2, :], slot[:, 1:2], tacc[:, 1, :],
                                                 ALU.is_le, ALU.add))
                eng.engine_nop().then_inc(s_cb, 1)

            for i in range(NB + 4):
                if 1 <= i <= NB:
                    evac_t(i - 1, 0)
                    evac_t(i - 1, 1)
                if 2 <= i <= NB + 1:
                    route(i - 2)
                    eng.engine_nop().then_inc(s_rt, 1)
                if 3 <= i <= NB + 2:
                    weigh(i - 3)
                if i >= 4:
                    tiles(i - 4)
            eng.tensor_scalar(t128[:, :, :], tacc[:, :, :], float(P), None, ALU.mult)
            ch.link(eng.tensor_tensor(rowi[:, :].rearrange("p (c e) -> p c e", c=2), tacc[:, :, :], e32[:, :, :],
                                      ALU.add))
            eng.engine_nop().then_inc(s_idx, 1)

            def split(k, e):
                n = pos[(k, e)]
                eng.wait_ge(s_H, n + 1)
                eng.tensor_tensor(LR[:, n % NHL, :], raw[:, n % NRAW, :], HR[:, n % NHL, :].bitcast(F32),
                                  ALU.subtract).then_inc(s_L, 1)

            def low_x(e, j):
                q = fq[("x", e, j)]
                c, h = divmod(j, 2)
                eng.wait_ge(s_fh, q + 1)
                eng.tensor_tensor(XL[:, e % 2, c, 4 * h:4 * h + 4, :].rearrange("p k n -> p (k n)"),
                                  bank(6 + q % 2),
                                  XH[:, e % 2, c, 4 * h:4 * h + 4, :].rearrange("p k n -> p (k n)").bitcast(F32),
                                  ALU.subtract).then_inc(s_fl, 1)

            def low_h(e, c):
                q = fq[("h", e, c)]
                eng.wait_ge(s_fh, q + 1)
                eng.tensor_tensor(hL[:, c, :, :].rearrange("p k n -> p (k n)"), bank(6 + q % 2, 0, I),
                                  hH[:, c, :, :].rearrange("p k n -> p (k n)").bitcast(F32),
                                  ALU.subtract).then_inc(s_fl, 1)

            def product(e, c):
                eng.wait_ge(s_sl, 2 * e + c + 1)
                if e:
                    eng.wait_ge(s_f, fq[("h", e - 1, c)] + 1)
                eng.tensor_tensor(prod[:, c, :, :].rearrange("q j p -> q p j"),
                                  sil[:, c, :].rearrange("q (p j) -> q p j", j=3),
                                  bank(2 * c + 1, 0, I).rearrange("q (p j) -> q p j", j=3),
                                  ALU.mult).then_inc(s_hp, 1)

            def token(e):
                eng.wait_ge(d_g[e % 2], 32 * (e // 2 + 1))
                for c in range(2):
                    ch.link(eng.tensor_scalar(Gj[:, :], G[:, e % 2, c, :], slot[:, c:c + 1], None, ALU.is_le, ALU.add,
                                              accum_out=cnt[:, c:c + 1]))
                    i = c * E + e
                    eng.tensor_scalar(toki[:, i:i + 1], t128[:, c, e:e + 1], cnt[:, c:c + 1], dum[:, c:c + 1],
                                      ALU.add, ALU.min).then_inc(s_tok, 1)

            def column(e):
                eng.wait_ge(d_xg[e % 2], 32 * (e // 2 + 1))
                for c in range(2):
                    ins = eng.tensor_copy(wcol[:, c * E + e:c * E + e + 1], Xg[:, e % 2, c, D + e:D + e + 1])
                    if c == 0:
                        ch.link(ins)
                ins.then_inc(s_wc, 1)

            for e in range(3):
                token(e)
            for k in ("gA", "uA", "gB", "uB"):
                split(k, 0)
            column(0)
            for j in range(4):
                low_x(0, j)
            for e in range(E + 1):
                if e >= 1:
                    low_h(e - 1, 0)
                    low_h(e - 1, 1)
                if e + 1 < E:
                    split("gA", e + 1)
                    split("uA", e + 1)
                    low_x(e + 1, 0)
                    low_x(e + 1, 1)
                    column(e + 1)
                    split("gB", e + 1)
                    split("uB", e + 1)
                    low_x(e + 1, 2)
                    low_x(e + 1, 3)
                if e + 3 < E:
                    token(e + 3)
                if e < E:
                    product(e, 0)
                    product(e, 1)
                    split("dA", e)
                    split("dB", e)

            eng.wait_ge(s_bh, 1)
            eng.tensor_tensor(BL[:, :, D + NA:NX], laR[:, :, :, :].rearrange("p q a r -> p q (a r)"),
                              BH[:, :, D + NA:NX].bitcast(F32), ALU.subtract).then_inc(s_bl, 1)
            for n in range(17):
                eng.wait_ge(s_bh, n + 2)
                if n == 0:
                    ins = eng.tensor_tensor(BL[:, :, D:D + NA], bank(6, 0, 64).rearrange("p (q a) -> p q a", q=8),
                                            BH[:, :, D:D + NA].bitcast(F32), ALU.subtract)
                else:
                    j, f = divmod(n - 1, 2)
                    a = (slice(None), slice(4 * f, 4 * f + 4), slice(j * P, (j + 1) * P))
                    ins = eng.tensor_tensor(BL[a], bank(6 + n % 2).rearrange("p (q n) -> p q n", q=4),
                                            BH[a].bitcast(F32), ALU.subtract)
                ins.then_inc(s_bl, 1)

            def low_w(k):
                eng.wait_ge(s_wh, k + 1)
                src = wr[:, k % 2, :, :] if k < 8 else bmR[:, :, :, :].rearrange("p q a r -> p q (a r)")
                eng.tensor_tensor(WL[:, k % 2, :, :], src, WH[:, k % 2, :, :].bitcast(F32), ALU.subtract)\
                   .then_inc(s_wl, 1)

            def low_m(k):
                eng.wait_ge(s_mh, k + 1)
                b0 = 3 * (k % 2)
                eng.tensor_tensor(ML[:, k, 0:768].rearrange("p (g n) -> p g n", g=2), ps[:, b0:b0 + 2, 0:384],
                                  MH[:, k, 0:768].rearrange("p (g n) -> p g n", g=2).bitcast(F32), ALU.subtract)
                eng.tensor_tensor(ML[:, k, 768:NX], bank(b0 + 2, 0, NX - 768), MH[:, k, 768:NX].bitcast(F32),
                                  ALU.subtract).then_inc(s_ml, 1)

            low_w(0)
            low_w(1)
            for k in range(9):
                low_m(k)
                if k + 2 < 9:
                    low_w(k + 2)

            eng.wait_ge(s_lbh, 1)
            eng.tensor_tensor(lbL[:, :], lb[:, :], lbH[:, :].bitcast(F32), ALU.subtract).then_inc(s_lbl, 1)
            eng.memset(z2[:, 8:14], 1e30).then_inc(s_pad, 1)
            for f in range(2):
                eng.wait_ge(s_ath, f + 1)
                eng.tensor_tensor(ATL[:, 4 * f:4 * f + 4, :].rearrange("p k n -> p (k n)"), bank(6 + f),
                                  ATH[:, 4 * f:4 * f + 4, :].rearrange("p k n -> p (k n)").bitcast(F32),
                                  ALU.subtract).then_inc(s_atl, 1)

            def low_t(t, f):
                eng.wait_ge(s_xh, 2 * t + f + 1)
                g, o = t // 2, (t % 2) * P
                a = (slice(None), g % 2, slice(4 * f, 4 * f + 4), slice(o, o + P))
                eng.tensor_tensor(xTL[a], bank(6).rearrange("p (k n) -> p k n", k=4), xTH[a].bitcast(F32),
                                  ALU.subtract).then_inc(s_xl, 1)

            def low_a(g):
                for o in range(2):
                    b = 2 * g + o
                    eng.wait_ge(s_xah, 2 * g + 2)
                    a = (slice(None), g % 2, slice(o * P, (o + 1) * P))
                    eng.scalar_tensor_tensor(xaL[a], bank(7, o * P, (o + 1) * P), mk[:, b:b + 1], xaH[a].bitcast(F32),
                                             ALU.mult, ALU.subtract).then_inc(s_xal, 1)

            def gate_of(t):
                b2 = 3 * (t % 2) + 2
                eng.wait_ge(s_mm, t + 1)
                if t == 0:
                    eng.wait_ge(d_bi, 32)
                    eng.wait_ge(s_pad, 1)
                ch.link(eng.tensor_tensor(lg2[:, :], bank(b2, 256, 264), rb[:, :], ALU.add))
                ch.link(eng.tensor_reduce(mx2[:, :], lg2[:, :], AX_X, ALU.max))
                if t:
                    eng.wait_ge(s_e2, t)
                ch.link(eng.tensor_scalar(z2[:, 0:NA], lg2[:, :], mx2[:, 0:1], ZMIN, ALU.subtract, ALU.max))
                eng.engine_nop().then_inc(s_z2, 1)
                ch.link(eng.max(t8[:, :], z2[:, :]))
                ch.link(eng.match_replace(zr2[:, :], t8[:, :], z2[:, :], 1.0))
                eng.wait_ge(s_e2, t + 1)
                ch.link(eng.scalar_tensor_tensor(g2[:, :], zr2[:, 0:NA], 0.5, e2[:, t % 2, :], ALU.is_ge, ALU.mult,
                                                 accum_out=sm2[:, 0:1]))
                ch.link(eng.reciprocal(sm2[:, 1:2], sm2[:, 0:1]))
                ch.link(eng.tensor_scalar(gate[:, :], g2[:, :], sm2[:, 1:2], 2.0, ALU.mult, ALU.mult))
                if t:
                    eng.wait_ge(s_mt, t)
                eng.tensor_tensor(mg[:, :].rearrange("p (a r) -> p a r", a=NA),
                                  bank(b2, 264, 392).rearrange("p (a r) -> p a r", a=NA),
                                  gate[:, :].unsqueeze(2).to_broadcast([P, NA, R]), ALU.mult).then_inc(s_mg, 1)

            def low_g(t):
                eng.wait_ge(s_mth, t + 1)
                eng.tensor_tensor(mgL[:, :], bank(7, 256, 384), mgH[:, :].bitcast(F32), ALU.subtract)\
                   .then_inc(s_mtl, 1)

            def final(t):
                b0, s = 3 * (t % 2), t % 6
                eng.wait_ge(s_lo, t + 1)
                eng.wait_ge(s_pb, t + 1)
                if t >= 3:
                    eng.wait_ge(d_o[t % 3], 16 * (t // 3))
                eng.tensor_tensor(osb[:, t % 3, 0:768].rearrange("p (g n) -> p g n", g=2), ps[:, b0:b0 + 2, 0:384],
                                  x1[:, s, 0:768].rearrange("p (g n) -> p g n", g=2), ALU.add).then_inc(s_fin, 1)
                eng.tensor_tensor(osb[:, t % 3, 768:D], bank(b0 + 2, 0, 256), x1[:, s, 768:D],
                                  ALU.add).then_inc(s_fin, 1)

            for t in range(2):
                for f in range(2):
                    low_t(t, f)
            low_a(0)
            for t in range(NB):
                if t:
                    gate_of(t - 1)
                if t + 2 < NB:
                    low_t(t + 2, 0)
                if t:
                    low_g(t - 1)
                if t + 2 < NB:
                    low_t(t + 2, 1)
                if t:
                    final(t - 1)
                if t % 2 and t + 1 < NB:
                    low_a(t // 2 + 1)
            gate_of(NB - 1)
            low_g(NB - 1)
            final(NB - 1)


_INS = ["x", "itok_B_1_198", "itok_B_0_6", "L0_cond_weights", "L0_ffn_gate_w", "L0_ffn_wg", "L0_ffn_wu", "L0_ffn_wd",
        "L1_cond_W", "L1_cond_A", "L1_cond_Bm", "L1_cond_scalings", "L1_ffn_base_w", "L1_ffn_base_b",
        "L1_ffn_router_w", "L1_ffn_router_b", "L1_ffn_lora_A", "L1_ffn_lora_B"]


def kernel(**inputs):
    import numpy as _np
    import concourse.bacc as _bacc
    from concourse import mybir as _mybir
    from concourse.bass_utils import run_bass_kernel_spmd as _run

    nc = _bacc.Bacc("TRN2", target_bir_lowering=False, num_devices=1)
    arrays, args = {}, []
    for name in _INS:
        a = _np.ascontiguousarray(inputs[name])
        arrays[f"in_{name}"] = a
        args.append(nc.dram_tensor(f"in_{name}", a.shape, _mybir.dt.from_np(a.dtype), kind="ExternalInput").ap())
    o = nc.dram_tensor("out_0", (32, 128, 1024), _mybir.dt.float32, kind="ExternalOutput").ap()
    adaln_ffn_kernel(nc, *args, o)
    r = _run(nc, [arrays], core_ids=[0])
    return r.results[0]["out_0"]
```

```python
from contextlib import ExitStack

import concourse.bass as bass
from concourse import mybir

F32 = mybir.dt.float32
F32R = mybir.dt.float32r
BF16 = mybir.dt.bfloat16
I32 = mybir.dt.int32
ALU = mybir.AluOpType
ACT = mybir.ActivationFunctionType
AX_X = mybir.AxisListType.X

P = 128
NB = 32
D = 1024
E = 64
I = 384
CAP = 256
TOK = NB * P
NA = 8
R = 16
NX = D + NA + NA * R
CG = [(0, 384), (384, 768), (768, NX)]
UN = 1536
NRAW = 4
NHL = 8
NY = 4
NS = 20
ZMIN = -87.8


class Count:

    def __init__(self, eng, sem):
        self.eng, self.sem, self.n = eng, sem, 0

    def mark(self, ins):
        self.n += 1
        ins.then_inc(self.sem, 1)
        return self.n

    def link(self, ins):
        self.eng.wait_ge(self.sem, self.mark(ins))


def adaln_ffn_kernel(nc, x, cond, adap, w0, gate_w, wg, wu, wd, W, A, Bm, scal,
                     base_w, base_b, router_w, router_b, lora_A, lora_B, out):
    x_r = x.rearrange("b c t -> (b c) t")
    out_r = out.rearrange("b c t -> (b c) t")
    w0_r = w0.rearrange("s c d -> (s c) d")
    yd = nc.dram_tensor("yd", (TOK + 2 * P, D), F32, kind="Internal").ap()
    yd4 = yd.rearrange("t (f s) -> (t f) s", f=4)
    wdr = nc.dram_tensor("wdr", (TOK + 2 * P, E), F32, kind="Internal").ap()
    acc = nc.dram_tensor("accd", (TOK + 2 * P, D), F32, kind="Internal").ap()
    tab = nc.dram_tensor("tabd", (E * NB + 1, P), F32, kind="Internal").ap()
    tab_v = tab[0:E * NB, :].rearrange("(e i) t -> i e t", i=NB)

    with ExitStack() as ctx:
        def sb(name, shape, dt, stack=None):
            return (stack or ctx).enter_context(nc.sbuf_tensor(name, shape, dt))

        def sem(name):
            return ctx.enter_context(nc.semaphore(name))

        ps = ctx.enter_context(nc.psum_tensor("ps", [P, 8, 512], F32))

        def bank(b, a=0, z=512, p=P):
            return ps[0:p, b, a:z]

        ident = sb("ident", [P, P], F32)
        tri = sb("tri", [P, P], BF16)
        ones = sb("ones", [P, P], BF16)
        slot = sb("slot", [P, 2], F32)
        dum = sb("dum", [P, 2], F32)
        pf = sb("pf", [P, 1], F32)
        t128 = sb("t128", [P, 2, E], F32)
        rowi = sb("rowi", [P, 2 * E], I32)
        toki = sb("toki", [P, 2 * E], I32)
        wcol = sb("wcol", [P, 2 * E], F32)
        mk = sb("mk", [P, NB], F32)
        f4 = sb("f4", [P, 1], F32)
        rep = sb("rep", [P, P], F32)
        qm = sb("qm", [P, 4, 2], F32)
        laR = sb("laR", [P, 8, NA, R], F32)
        bmR = sb("bmR", [P, 8, NA, R], F32)

        moe = ExitStack()
        raw = sb("raw", [P, NRAW, UN], F32, moe)
        HR = sb("HR", [P, NHL, UN], F32R, moe)
        LR = sb("LR", [P, NHL, UN], F32R, moe)

        rt = ExitStack()
        wall = sb("wall", [P, 16, P], F32, rt)
        xt = sb("xt", [P, 4, D], F32, rt)
        yrow = sb("yrow", [P, NY, D], F32, rt)
        wy = sb("wy", [P, NB, E], F32, rt)
        yT = sb("yT", [P, 2, 8, P], F32, rt)
        gT = sb("gT", [P, 8, P], F32, rt)
        gw = raw[0:E, 0, 0:D]
        gwp = raw[0:E, 1, 0:D]
        zrow = sb("zrow", [P, 256], F32, rt)
        e32 = sb("e32", [P, 2, E], F32, rt)
        tacc = sb("tacc", [P, 2, E], F32, rt)
        condi = sb("condi", [P, NB], I32, rt)
        adi = sb("adi", [P, NB], I32, rt)
        cidx = sb("cidx", [P, NB], I32, rt)
        scp = sb("scp", [P, 1], F32, rt)
        mkt = sb("mkt", [P, 3, NB], F32, rt)
        lgs = sb("lgs", [P, 4, E], F32, rt)
        m8 = sb("m8", [P, 4, 8], F32, rt)
        z8 = sb("z8", [P, 4, 8], F32, rt)
        zz = sb("zz", [P, 4, E], F32, rt)
        zr = sb("zr", [P, 4, E], F32, rt)
        eb = sb("eb", [P, 4, E], F32, rt)
        wm = sb("wm", [P, 4, E], F32, rt)
        sm = sb("sm", [P, 4], F32, rt)
        rc = sb("rc", [P, 4], F32, rt)
        mask = sb("mask", [P, 4, E], BF16, rt)
        macc = sb("macc", [P, 4, E], BF16, rt)
        ct = sb("ct", [E, 4, P], F32, rt)
        cb = sb("cb", [P, 4, E], F32, rt)
        rt.close()

        Xg = sb("Xg", [P, 2, 4, 256], F32, moe)
        XR = sb("XR", [P, 2, 4, 8, 32], F32, moe)
        Wg = sb("Wg", [P, 2, 2, E], F32, moe)
        tokf = sb("tokf", [P, 4, 2], F32, moe)
        tokq = sb("tokq", [P, 4, 8], F32, moe)
        idx4 = sb("idx4", [P, 4, 8], I32, moe)
        XH = sb("XH", [P, 2, 2, 8, P], F32R, moe)
        XL = sb("XL", [P, 2, 2, 8, P], F32R, moe)
        sil = sb("sil", [P, 2, I], F32, moe)
        prod = sb("prod", [P, 2, 3, P], F32, moe)
        hH = sb("hH", [P, 2, 3, P], F32R, moe)
        hL = sb("hL", [P, 2, 3, P], F32R, moe)
        G = sb("G", [P, 2, 2, P], F32, moe)
        Gj = sb("Gj", [P, 2, P], F32, moe)
        cnt = sb("cnt", [P, 2], F32, moe)
        ot = sb("ot", [P, 2, D], F32, moe)
        moe.close()

        x1 = sb("x1", [P, 6, D], F32)
        MH = sb("MH", [P, 9, NX], F32R)
        ML = sb("ML", [P, 9, NX], F32R)
        pre = ExitStack()
        WH = sb("WH", [P, 2, 8, P], F32R, pre)
        WL = sb("WL", [P, 2, 8, P], F32R, pre)
        BH = sb("BH", [P, 8, NX], F32R, pre)
        BL = sb("BL", [P, 8, NX], F32R, pre)
        pre.close()
        ar, lb = x1[:, 4, :], x1[:, 5, :]

        def wr(k):
            return x1[:, 2 + k % 2, :].rearrange("p (q d) -> p q d", q=8)

        xTH = sb("xTH", [P, 2, 8, 2 * P], F32R)
        xTL = sb("xTL", [P, 2, 8, 2 * P], F32R)
        ATH = sb("ATH", [P, 8, P], F32R)
        ATL = sb("ATL", [P, 8, P], F32R)
        lbH = sb("lbH", [P, D], F32R)
        lbL = sb("lbL", [P, D], F32R)
        bias = sb("bias", [P, D], F32)
        rb = sb("rb", [P, NA], F32)
        xaH = sb("xaH", [P, 2, 2 * P], F32R)
        xaL = sb("xaL", [P, 2, 2 * P], F32R)
        lg2 = sb("lg2", [P, NA], F32)
        mx2 = sb("mx2", [P, 1], F32)
        z2 = sb("z2", [P, 14], F32)
        t8 = sb("t8", [P, 8], F32)
        zr2 = sb("zr2", [P, 14], F32)
        e2 = sb("e2", [P, 2, NA], F32)
        g2 = sb("g2", [P, NA], F32)
        sm2 = sb("sm2", [P, 2], F32)
        gate = sb("gate", [P, NA], F32)
        mg = sb("mg", [P, P], F32)
        mgH = sb("mgH", [P, P], F32R)
        mgL = sb("mgL", [P, P], F32R)
        osb = sb("osb", [P, 3, D], F32)

        d_small, d_bc, d_gw, d_la = sem("d_small"), sem("d_bc"), sem("d_gw"), sem("d_la")
        d_z, d_ad = sem("d_z"), sem("d_ad")
        d_x = [sem(f"d_x{i}") for i in range(4)]
        d_as = [sem(f"d_as{i}") for i in range(4)]
        d_ys = [sem(f"d_ys{i}") for i in range(NY)]
        d_ts = [sem(f"d_ts{i}") for i in range(4)]
        d_wy = sem("d_wy")
        s_lgc = sem("s_lgc")
        d_w = [sem(f"d_w{i}") for i in range(4)]
        s_pc, s_cst, s_cidx, s_dv, s_zr = sem("s_pc"), sem("s_cst"), sem("s_cidx"), sem("s_dv"), sem("s_zr")
        s_gt, s_gte = sem("s_gt"), sem("s_gte")
        s_Y, s_yr, s_T, s_yT, s_lg = sem("s_Y"), sem("s_yr"), sem("s_T"), sem("s_yT"), sem("s_lg")
        s_z, s_e, s_wy, s_mask, s_cum = sem("s_z"), sem("s_e"), sem("s_wy"), sem("s_mask"), sem("s_cum")
        s_cte, s_cb, s_idx = sem("s_cte"), sem("s_cb"), sem("s_idx")
        d_raw = [sem(f"d_raw{i}") for i in range(NRAW)]
        s_H, s_L, s_k, s_dn = sem("s_H"), sem("s_L"), sem("s_k"), sem("s_dn")
        s_f, s_fh, s_fl = sem("s_f"), sem("s_fh"), sem("s_fl")
        s_sl, s_hp, s_out, s_tok, s_wc = sem("s_sl"), sem("s_hp"), sem("s_out"), sem("s_tok"), sem("s_wc")
        d_g = [sem(f"d_g{i}") for i in range(2)]
        d_xg = [sem(f"d_xg{i}") for i in range(2)]
        d_wg = [sem(f"d_wg{i}") for i in range(2)]
        s_vt, s_vh, s_vl, s_i4, s_gwp = sem("s_vt"), sem("s_vh"), sem("s_vl"), sem("s_i4"), sem("s_gwp")
        d_sc = sem("d_sc")
        d_bw = [sem(f"d_bw{i}") for i in range(2)]
        d_wr = [sem(f"d_wr{i}") for i in range(2)]
        s_bf, s_bh, s_bl, s_wh, s_wl = sem("s_bf"), sem("s_bh"), sem("s_bl"), sem("s_wh"), sem("s_wl")
        s_m, s_mh, s_ml = sem("s_m"), sem("s_mh"), sem("s_ml")
        d_ab, d_bi = sem("d_ab"), sem("d_bi")
        d_x1 = [sem(f"d_x1{i}") for i in range(6)]
        d_o = [sem(f"d_o{i}") for i in range(3)]
        s_at, s_ath, s_atl, s_lbh, s_lbl = sem("s_at"), sem("s_ath"), sem("s_atl"), sem("s_lbh"), sem("s_lbl")
        s_xf, s_xh, s_xl = sem("s_xf"), sem("s_xh"), sem("s_xl")
        s_xa, s_xah, s_xal = sem("s_xa"), sem("s_xah"), sem("s_xal")
        s_mm, s_z2, s_e2, s_mg, s_mt, s_mth, s_mtl = [sem(n) for n in ("s_mm", "s_z2", "s_e2", "s_mg", "s_mt", "s_mth", "s_mtl")]
        s_lo, s_fin, s_pb, s_pad = sem("s_lo"), sem("s_fin"), sem("s_pb"), sem("s_pad")

        units, pos = [], {}

        def stream(kinds, e):
            for k in kinds:
                pos[(k, e)] = len(units)
                units.append((k, e))

        stream(["gA", "uA", "gB", "uB"], 0)
        for e in range(1, E):
            stream(["gA", "uA", "gB", "uB"], e)
            stream(["dA", "dB"], e - 1)
        stream(["dA", "dB"], E - 1)

        def unit_src(n):
            k, e = units[n]
            h = 0 if k[1] == "A" else UN
            if k[0] == "d":
                v = wd[e].rearrange("(p j) h -> p (j h)", j=3)
            else:
                v = (wg if k[0] == "g" else wu)[e].rearrange("(p k) i -> p (k i)", k=8)
            return v[:, h:h + UN]

        def wait_retired(eng, n):
            k, e = units[n]
            if k[0] == "d":
                eng.wait_ge(s_dn, 4 * (e + 1))
            else:
                eng.wait_ge(s_k, 2 * e + (1 if k[1] == "A" else 2))

        BF = [6, 7, 0, 1, 2, 3, 4, 5]

        fq = {}
        for e in range(2):
            fq[("i", e)] = len(fq)
        for e in range(E):
            if e + 2 < E:
                fq[("i", e + 2)] = len(fq)
            for c in range(2):
                fq[("h", e, c)] = len(fq)

        def bcast(ap1, n):
            return ap1.rearrange("(a n) -> a n", a=1).to_broadcast([P, n])

        block = ctx.enter_context(nc.Block())

        @block.sync
        def _(eng):
            eng.dma_start(condi[:, :], bcast(cond, NB)).then_inc(d_small, 16)
            eng.dma_start(gw, gate_w).then_inc(d_gw, 16)
            eng.dma_start(adi[:, :], bcast(adap, NB)).then_inc(d_bc, 16)
            for a in range(NA):
                eng.dma_start(scp[R * a:R * a + R, :],
                              scal[a:a + 1].rearrange("(a n) -> a n", a=1).to_broadcast([R, 1])).then_inc(d_bc, 16)

            def load_unit(n):
                if n >= NRAW:
                    eng.wait_ge(s_L, n - NRAW + 1)
                eng.dma_start(raw[:, n % NRAW, :], unit_src(n)).then_inc(d_raw[n % NRAW], 16)

            for i in range(NB + 1):
                if i < NB:
                    if i >= 4:
                        eng.wait_ge(s_Y, 2 * (i - 3))
                        if i < NS + 4:
                            eng.wait_ge(d_as[i % 4], 16 * (i // 4))
                    eng.dma_start(xt[:, i % 4, :], x_r[i * P:(i + 1) * P, :]).then_inc(d_x[i % 4], 16)
                if i == 3:
                    eng.wait_ge(s_zr, 1)
                    for c in range(2):
                        r0 = TOK + c * P
                        for q in range(4):
                            eng.dma_start(yd[r0:r0 + P, q * 256:(q + 1) * 256], zrow[:, :]).then_inc(d_z, 16)
                            eng.dma_start(acc[r0:r0 + P, q * 256:(q + 1) * 256], zrow[:, 0:256]).then_inc(d_z, 16)
                        eng.dma_start(wdr[r0:r0 + P, :], zrow[:, 0:E]).then_inc(d_z, 16)
                    eng.dma_start(tab[E * NB:E * NB + 1, :], zrow[0:1, 0:P]).then_inc(d_z, 16)
                if 1 <= i <= NS:
                    j = i - 1
                    eng.wait_ge(d_x[j % 4], 16 * (j // 4 + 1))
                    eng.dma_start(acc[j * P:(j + 1) * P, :], xt[:, j % 4, :]).then_inc(d_as[j % 4], 16)
                if i >= 24 and i % 2 == 0 and i < 24 + 2 * NRAW:
                    load_unit((i - 24) // 2)
            for i in range(NS, NB, 4):
                eng.dma_start(acc[i * P:(i + 4) * P, :], x_r[i * P:(i + 4) * P, :]).then_inc(d_ad, 16)
            for n in range(NRAW, len(units)):
                load_unit(n)
                if n >= 100 and n % 4 == 0 and n < 100 + 4 * NA:
                    e = (n - 100) // 4
                    with nc.allow_non_contiguous_dma(reason="64-byte rows"):
                        eng.dma_start(laR[:, :, e, :],
                                      lora_A[e].rearrange("(q p) r -> p q r", p=P)).then_inc(d_la, 16)
                        eng.dma_start(bmR[:, :, e, :],
                                      Bm[e].rearrange("(q p) r -> p q r", p=P)).then_inc(d_la, 16)

            eng.wait_ge(s_L, len(units))
            eng.dma_start(x1[0:NA, 0, :], router_w).then_inc(d_bw[0], 16)
            eng.dma_start(x1[:, 1, :], base_w[0:P, :]).then_inc(d_bw[1], 16)

            def load_w(k):
                eng.dma_start(wr(k), W.rearrange("(q p) d -> p q d", p=P)[:, :, k * P:(k + 1) * P])\
                   .then_inc(d_wr[k % 2], 16)

            load_w(0)
            load_w(1)
            for j in range(1, 8):
                eng.wait_ge(s_bf, 1 + 2 * (j - 1))
                eng.dma_start(x1[:, (j + 1) % 2, :], base_w[j * P:(j + 1) * P, :]).then_inc(d_bw[(j + 1) % 2], 16)
            eng.dma_start(ar, A.rearrange("a r d -> (a r) d")).then_inc(d_ab, 16)
            eng.dma_start(lb, lora_B.rearrange("e r d -> (e r) d")).then_inc(d_ab, 16)
            for k in range(2, 8):
                eng.wait_ge(s_wl, k - 1)
                load_w(k)

            def load_x(t):
                eng.dma_start(x1[:, t % 6, :], acc[t * P:(t + 1) * P, :]).then_inc(d_x1[t % 6], 16)

            eng.wait_ge(d_sc, 32 * E)
            eng.wait_ge(s_bf, 17)
            load_x(0)
            load_x(1)
            eng.wait_ge(s_wl, 8)
            load_x(2)
            load_x(3)
            eng.wait_ge(s_m, 9)
            eng.dma_start(bias[:, :], bcast(base_b, D)).then_inc(d_bi, 16)
            eng.dma_start(rb[:, :], bcast(router_b, NA)).then_inc(d_bi, 16)
            eng.wait_ge(s_at, 2)
            eng.wait_ge(s_lbl, 1)
            for t in range(4, NB + 6):
                if t >= 6:
                    eng.wait_ge(s_fin, 2 * (t - 5))
                    eng.dma_start(out_r[(t - 6) * P:(t - 5) * P, :], osb[:, t % 3, :]).then_inc(d_o[t % 3], 16)
                if t < NB:
                    eng.dma_start(x1[:, t % 6, :], acc[t * P:(t + 1) * P, :]).then_inc(d_x1[t % 6], 16)
            for s in range(3):
                eng.wait_ge(d_o[s], 16 * len(range(s, NB, 3)))

        @block.gpsimd
        def _(eng):
            ch = Count(eng, s_pc)
            eng.memset(ident[:, :], 0.0)
            eng.memset(ones[:, :], 1.0)
            eng.memset(rep[:, :], 0.0)
            ch.link(eng.memset(tri[:, :], 1.0))
            eng.affine_select(out=ident[:, :], in_=ident[:, :], compare_op=ALU.not_equal, fill=1.0,
                              base=0, pattern=[[-1, P]], channel_multiplier=1)
            eng.affine_select(out=tri[:, :], in_=tri[:, :], compare_op=ALU.is_ge, fill=0.0,
                              base=0, pattern=[[1, P]], channel_multiplier=-1)
            v = rep[:, :].rearrange("p (f t) -> p f t", f=4)
            for q in range(4):
                ch.link(eng.affine_select(out=v, in_=v, compare_op=ALU.not_equal, fill=1.0,
                                          base=-32 * q, pattern=[[0, 4], [-1, 32]], channel_multiplier=1))
            eng.iota(pf[:, :], [[0, 1]], base=0, channel_multiplier=1, allow_small_or_imprecise_dtypes=True)
            eng.iota(slot[:, :], [[P, 2]], base=0, channel_multiplier=1, allow_small_or_imprecise_dtypes=True)
            eng.iota(dum[:, :], [[P, 2]], base=TOK, channel_multiplier=1, allow_small_or_imprecise_dtypes=True)
            eng.iota(e32[:, :, :], [[0, 2], [NB, E]], base=0, channel_multiplier=0,
                     allow_small_or_imprecise_dtypes=True).then_inc(s_cst, 1)
            eng.wait_ge(s_cidx, 1)
            for b in range(NB):
                if b >= 16:
                    eng.wait_ge(s_Y, 2 * (b - 15))
                eng.indirect_dma_start(wall[:, b % 16, :], None, w0_r,
                                       bass.IndirectOffsetOnAxis(ap=cidx[:, b:b + 1], axis=0))\
                   .then_inc(d_w[b // 8], 16)

            def gather_tab(e):
                if e == 0:
                    for s in range(4):
                        eng.wait_ge(d_ts[s], 16 * (NB // 4))
                    eng.wait_ge(d_z, 16 * 19)
                    eng.wait_ge(s_idx, 1)
                if e >= 2:
                    eng.wait_ge(s_tok, 2 * (e - 1))
                for c in range(2):
                    eng.indirect_dma_start(G[:, e % 2, c, :], None, tab,
                                           bass.IndirectOffsetOnAxis(ap=rowi[:, c * E + e:c * E + e + 1], axis=0))\
                       .then_inc(d_g[e % 2], 16)

            def gather_x(e):
                eng.wait_ge(s_i4, e + 1)
                if e == 0:
                    eng.wait_ge(d_wy, 16 * NB // 4)
                    for s in range(NY):
                        eng.wait_ge(d_ys[s], 16 * len(range(s, NB, NY)))
                    for s in range(4):
                        eng.wait_ge(d_as[s], 16 * (NS // 4))
                for c in range(2):
                    if e:
                        eng.wait_ge(s_vt, 2 * (e - 1) + c + 1)
                    for q in range(4):
                        i = 2 * q + c
                        eng.indirect_dma_start(Xg[:, c, q, :], None, yd4,
                                               bass.IndirectOffsetOnAxis(ap=idx4[:, e % 4, i:i + 1], axis=0))\
                           .then_inc(d_xg[c], 16)

            def gather_w(e):
                if e >= 2:
                    eng.wait_ge(s_wc, e - 1)
                else:
                    eng.wait_ge(d_wy, 16 * NB // 4)
                for c in range(2):
                    eng.indirect_dma_start(Wg[:, e % 2, c, :], None, wdr,
                                           bass.IndirectOffsetOnAxis(ap=toki[:, c * E + e:c * E + e + 1], axis=0))\
                       .then_inc(d_wg[e % 2], 16)

            def scatter(e):
                if e >= 1:
                    eng.wait_ge(d_sc, 32 * e)
                else:
                    eng.wait_ge(d_ad, 16 * ((NB - NS) // 4))
                for c in range(2):
                    eng.wait_ge(s_out, 4 * e + 2 * c + 2)
                    eng.indirect_dma_start(acc, bass.IndirectOffsetOnAxis(ap=toki[:, c * E + e:c * E + e + 1], axis=0),
                                           ot[:, c, :], None, compute_op=ALU.add).then_inc(d_sc, 16)

            gather_tab(0)
            gather_tab(1)
            gather_x(0)
            gather_x(1)
            gather_tab(2)
            gather_w(0)
            gather_w(1)
            for e in range(E + 1):
                if e + 3 < E:
                    gather_tab(e + 3)
                if e + 2 < E:
                    gather_x(e + 2)
                    gather_w(e + 2)
                if e >= 1:
                    scatter(e - 1)
            eng.wait_ge(d_sc, 32 * E)

            eng.wait_ge(d_bi, 32)
            for t in range(NB):
                eng.wait_ge(d_x1[t % 6], 16 * (t // 6 + 1))
                eng.wait_ge(s_xf, 2 * (t + 1))
                eng.tensor_tensor(x1[:, t % 6, :], x1[:, t % 6, :], bias[:, :], ALU.add).then_inc(s_pb, 1)

        @block.tensor
        def _(eng):
            eng.wait_ge(s_cst, 1)
            eng.wait_ge(s_gwp, 1)
            for k in range(8):
                mm = eng.transpose(bank(4, k * E, (k + 1) * E), gwp[:, k * P:(k + 1) * P], ident[0:E, 0:E])
            mm.then_inc(s_gt, 1)

            def condition(i):
                eng.wait_ge(d_w[i // 8], 16 * 8)
                eng.wait_ge(d_x[i % 4], 16 * (i // 4 + 1))
                for h in range(2):
                    if i:
                        eng.wait_ge(s_yr, 2 * i - 1 + h)
                    eng.matmul(bank(h), wall[:, i % 16, :], xt[:, i % 4, h * 512:(h + 1) * 512],
                               start=True, stop=True).then_inc(s_Y, 1)

            def turn(i):
                eng.wait_ge(s_yr, 2 * i + 2)
                for f in range(2):
                    n = 2 * i + f
                    if n >= 2:
                        eng.wait_ge(s_yT, n - 1)
                    for q in range(4):
                        k = 4 * f + q
                        mm = eng.transpose(bank(2 + f, q * P, (q + 1) * P), yrow[:, i % NY, k * P:(k + 1) * P],
                                           ident[:, :])
                    mm.then_inc(s_T, 1)

            def logits(i):
                if i == 0:
                    eng.wait_ge(s_gte, 1)
                eng.wait_ge(s_yT, 2 * i + 2)
                if i >= 2:
                    eng.wait_ge(s_lgc, i - 1)
                for k in range(8):
                    mm = eng.matmul(bank(4 + i % 2, 0, P), yT[:, i % 2, k, :], gT[:, k, :], start=(k == 0), stop=(k == 7))
                mm.then_inc(s_lg, 1)

            def counts(i):
                eng.wait_ge(s_mask, 2 * i + 2)
                if i >= 2:
                    eng.wait_ge(s_cte, i - 1)
                b = 6 + i % 2
                eng.matmul(bank(b, 0, P, E), mask[:, i % 4, :], tri[:, :], start=True, stop=(i == 0))
                if i:
                    eng.matmul(bank(b, 0, P, E), macc[:, (i - 1) % 4, :], ones[:, :], start=False, stop=True)
                eng.matmul(bank(b, P, P + E), ones[:, :], macc[:, i % 4, :], start=True, stop=True)\
                   .then_inc(s_cum, 1)

            for i in range(NB + 4):
                if i < NB:
                    condition(i)
                if 1 <= i <= NB:
                    turn(i - 1)
                if 2 <= i <= NB + 1:
                    logits(i - 2)
                if i >= 4:
                    counts(i - 4)

            def repeat(e):
                q = fq[("i", e)]
                if q >= 2:
                    eng.wait_ge(s_fl, q - 1)
                else:
                    eng.wait_ge(s_cte, NB)
                eng.wait_ge(s_tok, 2 * e + 2)
                eng.matmul(bank(6 + q % 2, 0, 8), rep[:, :], tokq[:, e % 4, :], start=True, stop=True)\
                   .then_inc(s_f, 1)

            def turn_h(e, c):
                q = fq[("h", e, c)]
                eng.wait_ge(s_fl, q - 1)
                eng.wait_ge(s_hp, 2 * e + c + 1)
                for j in range(3):
                    mm = eng.transpose(bank(6 + q % 2, j * P, (j + 1) * P), prod[:, c, j, :], ident[:, :])
                mm.then_inc(s_f, 1)

            def up(e):
                eng.wait_ge(s_vl, 2 * e + 2)
                if e >= 1:
                    eng.wait_ge(s_hp, 2 * e)
                for k in range(8):
                    half = "A" if k < 4 else "B"
                    n = pos[("u" + half, e)]
                    if k % 4 == 0:
                        eng.wait_ge(s_L, n + 1)
                    o = (k % 4) * I
                    gs, us = (n - 1) % NHL, n % NHL
                    for c in range(2):
                        ops = [(XH, HR, gs, 0), (XH, HR, us, 1), (XH, LR, gs, 0), (XH, LR, us, 1),
                               (XL, HR, gs, 0), (XL, HR, us, 1)]
                        for m, (X, Wt, s, g) in enumerate(ops):
                            mm = eng.matmul(bank(2 * c + g, 0, I), X[:, e % 2, c, k, :], Wt[:, s, o:o + I],
                                            start=(k == 0 and m < 2), stop=(k == 7 and m >= 4))
                    if k in (3, 7):
                        mm.then_inc(s_k, 1)
                    if k == (1 if e else 7) and e + 2 < E:
                        repeat(e + 2)

            def down(e):
                eng.wait_ge(s_fl, fq[("h", e, 1)] + 1)
                eng.wait_ge(s_L, pos[("dB", e)] + 1)
                for c in range(2):
                    for h in range(2):
                        o = 4 * e + 2 * c + h
                        if o >= 2:
                            eng.wait_ge(s_out, o - 1)
                        for j in range(3):
                            flat = j * D + h * 512
                            s = (pos[("dA", e)] + flat // UN) % NHL
                            f = flat % UN
                            for m, (X, Wt) in enumerate([(hH, HR), (hL, HR), (hH, LR)]):
                                mm = eng.matmul(bank(4 + h), X[:, c, j, :], Wt[:, s, f:f + 512],
                                                start=(j == 0 and m == 0), stop=(j == 2 and m == 2))
                        mm.then_inc(s_dn, 1)

            repeat(0)
            repeat(1)
            for e in range(E):
                up(e)
                if e >= 1:
                    down(e - 1)
                for c in range(2):
                    turn_h(e, c)
            down(E - 1)

            eng.wait_ge(s_hp, 2 * E)
            eng.wait_ge(s_fl, len(fq))
            eng.wait_ge(d_bw[0], 16)
            for q in range(8):
                mm = eng.transpose(bank(BF[0], q * NA, (q + 1) * NA), x1[0:NA, 0, q * P:(q + 1) * P],
                                   ident[0:NA, 0:NA])
            mm.then_inc(s_bf, 1)
            for j in range(8):
                s = (j + 1) % 2
                eng.wait_ge(d_bw[s], 16 * (1 + (j + 1) // 2 if s == 0 else j // 2 + 1))
                for f in range(2):
                    n = 1 + 2 * j + f
                    if n == 6:
                        eng.wait_ge(s_out, 4 * E)
                    if n >= 8:
                        eng.wait_ge(s_bl, n - 6)
                    for r in range(4):
                        q = 4 * f + r
                        mm = eng.transpose(bank(BF[n % 8], r * P, (r + 1) * P), x1[:, s, q * P:(q + 1) * P],
                                           ident[:, :])
                    mm.then_inc(s_bf, 1)
            eng.wait_ge(s_bl, 18)
            for k in range(9):
                eng.wait_ge(s_wl, k + 1)
                if k >= 2:
                    eng.wait_ge(s_ml, k - 1)
                b0 = 3 * (k % 2)
                for q in range(8):
                    for m, (X, Y) in enumerate([(WH, BH), (WH, BL), (WL, BH)]):
                        for g, (a, z) in enumerate(CG):
                            mm = eng.matmul(bank(b0 + g, 0, z - a), X[:, k % 2, q, :], Y[:, q, a:z],
                                            start=(q == 0 and m == 0), stop=(q == 7 and m == 2))
                mm.then_inc(s_m, 1)

            eng.wait_ge(d_ab, 32)
            for f in range(2):
                for r in range(4):
                    k = 4 * f + r
                    mm = eng.transpose(bank(6 + f, r * P, (r + 1) * P), ar[:, k * P:(k + 1) * P], ident[:, :])
                mm.then_inc(s_at, 1)

            def turn_t(t, f):
                n = 2 * t + f
                if f == 0:
                    eng.wait_ge(d_x1[t % 6], 16 * (t // 6 + 1))
                if n:
                    eng.wait_ge(s_xl, n)
                else:
                    eng.wait_ge(s_atl, 2)
                for r in range(4):
                    k = 4 * f + r
                    mm = eng.transpose(bank(6, r * P, (r + 1) * P), x1[:, t % 6, k * P:(k + 1) * P], ident[:, :])
                mm.then_inc(s_xf, 1)

            def adapter(g):
                eng.wait_ge(s_xl, 4 * (g + 1))
                if g:
                    eng.wait_ge(s_xal, 2 * g)
                    eng.wait_ge(s_mtl, 2 * g - 1)
                for k in range(8):
                    for m, (X, Y) in enumerate([(ATH, xTH), (ATH, xTL), (ATL, xTH)]):
                        mm = eng.matmul(bank(7, 0, 256), X[:, k, :], Y[:, g % 2, k, :],
                                        start=(k == 0 and m == 0), stop=(k == 7 and m == 2))
                mm.then_inc(s_xa, 1)

            def turn_m(t):
                eng.wait_ge(s_mg, t + 1)
                eng.wait_ge(s_xal, 2 * min((t + 1) // 2 + 1, NB // 2))
                if t:
                    eng.wait_ge(s_mtl, t)
                eng.transpose(bank(7, 256, 384), mg[:, :], ident[:, :]).then_inc(s_mt, 1)

            def lora(t):
                eng.wait_ge(s_mtl, t + 1)
                b0 = 3 * (t % 2)
                for m, (X, Y) in enumerate([(mgH, lbH), (mgH, lbL), (mgL, lbH)]):
                    for g, (a, z) in enumerate(CG):
                        z = min(z, D)
                        mm = eng.matmul(bank(b0 + g, 0, z - a), X[:, :], Y[:, a:z], start=False, stop=(m == 2),
                                        skip_group_check=True)
                mm.then_inc(s_lo, 1)

            for t in range(2):
                for f in range(2):
                    turn_t(t, f)
            adapter(0)
            for t in range(NB):
                g, o = t // 2, (t % 2) * P
                if t >= 2:
                    eng.wait_ge(s_fin, 2 * (t - 1))
                else:
                    eng.wait_ge(s_ml, 9)
                if t == 0:
                    eng.wait_ge(s_lbl, 1)
                b0 = 3 * (t % 2)
                for k in range(9):
                    if k == 8:
                        eng.wait_ge(s_xal, 2 * (g + 1))
                        ops = [(xaH[:, g % 2, o:o + P], MH), (xaH[:, g % 2, o:o + P], ML), (xaL[:, g % 2, o:o + P], MH)]
                    else:
                        xh, xl = xTH[:, g % 2, k, o:o + P], xTL[:, g % 2, k, o:o + P]
                        ops = [(xh, MH), (xh, ML), (xl, MH)]
                    for m, (X, Y) in enumerate(ops):
                        for n, (a, z) in enumerate(CG):
                            mm = eng.matmul(bank(b0 + n, 0, z - a), X, Y[:, k, a:z],
                                            start=(k == 0 and m == 0), stop=(k == 8 and m == 2))
                    if k == 8:
                        mm.then_inc(s_mm, 1)
                    if k in (2, 5) and t + 2 < NB:
                        turn_t(t + 2, (k - 2) // 3)
                    if k == 3 and t:
                        turn_m(t - 1)
                    if k == 6 and t:
                        lora(t - 1)
                if t % 2 and t + 1 < NB:
                    adapter(g + 1)
            turn_m(NB - 1)
            lora(NB - 1)

        @block.scalar
        def _(eng):
            def evac_y(i):
                if i >= NY:
                    eng.wait_ge(d_ys[i % NY], 16 * (i // NY))
                    eng.wait_ge(s_T, 2 * (i - NY) + 2)
                for h in range(2):
                    eng.wait_ge(s_Y, 2 * i + h + 1)
                    eng.activation(yrow[:, i % NY, :].rearrange("q (f j a) -> q f a j", f=4, j=8)[:, 2 * h:2 * h + 2],
                                   bank(h).rearrange("q (f a j) -> q f a j", f=2, j=8), ACT.Copy).then_inc(s_yr, 1)

            def store_y(i):
                eng.wait_ge(s_yr, 2 * i + 2)
                eng.dma_start(yd[i * P:(i + 1) * P, :], yrow[:, i % NY, :]).then_inc(d_ys[i % NY], 16)

            def copy_l(i):
                eng.wait_ge(s_lg, i + 1)
                if i >= 4:
                    eng.wait_ge(s_z, i - 3)
                eng.activation(lgs[:, i % 4, :], bank(4 + i % 2, 0, E), ACT.Copy).then_inc(s_lgc, 1)

            def exps(i):
                eng.wait_ge(s_z, i + 1)
                eng.activation(eb[:, i % 4, :], zz[:, i % 4, :], ACT.Exp).then_inc(s_e, 1)

            def copy_c(i):
                eng.wait_ge(s_cum, i + 1)
                if i >= 4:
                    eng.wait_ge(d_ts[i % 4], 16 * (i // 4))
                    eng.wait_ge(s_cb, i - 3)
                eng.activation(ct[:, i % 4, :], bank(6 + i % 2, 0, P, E), ACT.Copy)
                eng.activation(cb[:, i % 4, :], bank(6 + i % 2, P, P + E), ACT.Copy).then_inc(s_cte, 1)

            def store_c(i):
                eng.wait_ge(s_cte, i + 1)
                eng.dma_start(tab_v[i], ct[:, i % 4, :]).then_inc(d_ts[i % 4], 16)

            def store_w(i):
                eng.wait_ge(s_wy, i + 1)
                a = i - 3
                eng.dma_start(wdr[a * P:(i + 1) * P, :].rearrange("(b q) e -> q b e", q=P),
                              wy[:, a:i + 1, :]).then_inc(d_wy, 16)

            for i in range(NB + 8):
                if 3 <= i < NB + 3:
                    copy_l(i - 3)
                if 4 <= i < NB + 4:
                    exps(i - 4)
                if 5 <= i < NB + 5:
                    copy_c(i - 5)
                if i < NB:
                    evac_y(i)
                if 1 <= i <= NB:
                    store_y(i - 1)
                if 6 <= i < NB + 6:
                    store_c(i - 6)
                if i >= 8 and (i - 7) % 4 == 0:
                    store_w(i - 8)

            def split(k, e):
                n = pos[(k, e)]
                eng.wait_ge(d_raw[n % NRAW], 16 * (n // NRAW + 1))
                if n >= NHL:
                    wait_retired(eng, n - NHL)
                eng.activation(HR[:, n % NHL, :], raw[:, n % NRAW, :], ACT.Copy).then_inc(s_H, 1)

            def high_x(e, c):
                eng.wait_ge(s_vt, 2 * e + c + 1)
                eng.activation(XH[:, e % 2, c, :, :].rearrange("p j (q t) -> p q j t", q=4), XR[:, c, :, :, :],
                               ACT.Copy).then_inc(s_vh, 1)

            def high_h(e, c):
                q = fq[("h", e, c)]
                eng.wait_ge(s_f, q + 1)
                eng.activation(hH[:, c, :, :], bank(6 + q % 2, 0, I), ACT.Copy).then_inc(s_fh, 1)

            def silu(e, c):
                eng.wait_ge(s_k, 2 * e + 2)
                if e:
                    eng.wait_ge(s_hp, 2 * (e - 1) + c + 1)
                eng.activation(sil[:, c, :], bank(2 * c, 0, I), ACT.Silu).then_inc(s_sl, 1)

            def result(e, c, h):
                if e:
                    eng.wait_ge(d_sc, 32 * e)
                eng.wait_ge(s_wc, e + 1)
                eng.wait_ge(s_dn, 4 * e + 2 * c + h + 1)
                eng.activation(ot[:, c, h * 512:(h + 1) * 512], bank(4 + h), ACT.Copy,
                               scale=wcol[:, c * E + e:c * E + e + 1]).then_inc(s_out, 1)

            for k in ("gA", "uA", "gB", "uB"):
                split(k, 0)
            for c in range(2):
                high_x(0, c)
            for e in range(E + 1):
                if e >= 1:
                    high_h(e - 1, 0)
                    high_h(e - 1, 1)
                if e + 1 < E:
                    split("gA", e + 1)
                    high_x(e + 1, 0)
                    split("uA", e + 1)
                    high_x(e + 1, 1)
                    split("gB", e + 1)
                    split("uB", e + 1)
                if e < E:
                    silu(e, 0)
                    silu(e, 1)
                    split("dA", e)
                if e >= 1:
                    result(e - 1, 0, 0)
                    result(e - 1, 0, 1)
                if e < E:
                    split("dB", e)
                if e >= 1:
                    result(e - 1, 1, 0)
                    result(e - 1, 1, 1)

            eng.wait_ge(s_dn, 4 * E)
            eng.wait_ge(d_la, 16 * 16)

            def high_w(k):
                if k < 8:
                    eng.wait_ge(d_wr[k % 2], 16 * (k // 2 + 1))
                    src = wr(k)
                else:
                    src = bmR[:, :, :, :].rearrange("p q a r -> p q (a r)")
                if k >= 2:
                    eng.wait_ge(s_m, k - 1)
                eng.activation(WH[:, k % 2, :, :], src, ACT.Copy).then_inc(s_wh, 1)

            eng.activation(BH[:, :, D + NA:NX], laR[:, :, :, :].rearrange("p q a r -> p q (a r)"), ACT.Copy)\
               .then_inc(s_bh, 1)
            for n in range(17):
                eng.wait_ge(s_bf, n + 1)
                if n == 0:
                    eng.activation(BH[:, :, D:D + NA], bank(6, 0, 64).rearrange("p (q a) -> p q a", q=8), ACT.Copy)\
                       .then_inc(s_bh, 1)
                else:
                    j, f = divmod(n - 1, 2)
                    eng.activation(BH[:, 4 * f:4 * f + 4, j * P:(j + 1) * P],
                                   bank(BF[n % 8]).rearrange("p (q n) -> p q n", q=4), ACT.Copy).then_inc(s_bh, 1)

            def high_m(k):
                eng.wait_ge(s_m, k + 1)
                b0 = 3 * (k % 2)
                eng.activation(MH[:, k, 0:768].rearrange("p (g n) -> p g n", g=2), ps[:, b0:b0 + 2, 0:384], ACT.Copy)
                eng.activation(MH[:, k, 768:NX], bank(b0 + 2, 0, NX - 768), ACT.Copy).then_inc(s_mh, 1)

            high_w(0)
            high_w(1)
            for k in range(9):
                high_m(k)
                if k + 2 < 9:
                    high_w(k + 2)

            eng.wait_ge(d_ab, 32)
            eng.activation(lbH[:, :], lb, ACT.Copy).then_inc(s_lbh, 1)
            for f in range(2):
                eng.wait_ge(s_at, f + 1)
                eng.activation(ATH[:, 4 * f:4 * f + 4, :], bank(6 + f), ACT.Copy).then_inc(s_ath, 1)

            def high_t(t, f):
                eng.wait_ge(s_xf, 2 * t + f + 1)
                g, o = t // 2, (t % 2) * P
                eng.activation(xTH[:, g % 2, 4 * f:4 * f + 4, o:o + P], bank(6).rearrange("p (k n) -> p k n", k=4),
                               ACT.Copy).then_inc(s_xh, 1)

            def high_a(g):
                eng.wait_ge(s_xa, g + 1)
                for o in range(2):
                    b = 2 * g + o
                    eng.activation(xaH[:, g % 2, o * P:(o + 1) * P], bank(7, o * P, (o + 1) * P), ACT.Copy,
                                   scale=mk[:, b:b + 1]).then_inc(s_xah, 1)

            def exp2(t):
                eng.wait_ge(s_z2, t + 1)
                if t >= 2:
                    eng.wait_ge(s_mg, t - 1)
                eng.activation(e2[:, t % 2, :], z2[:, 0:NA], ACT.Exp).then_inc(s_e2, 1)

            def high_g(t):
                eng.wait_ge(s_mt, t + 1)
                if t:
                    eng.wait_ge(s_lo, t)
                eng.activation(mgH[:, :], bank(7, 256, 384), ACT.Copy).then_inc(s_mth, 1)

            for t in range(2):
                for f in range(2):
                    high_t(t, f)
            high_a(0)
            for t in range(NB):
                if t:
                    exp2(t - 1)
                if t + 2 < NB:
                    high_t(t + 2, 0)
                if t:
                    high_g(t - 1)
                if t + 2 < NB:
                    high_t(t + 2, 1)
                if t % 2 and t + 1 < NB:
                    high_a(t // 2 + 1)
            exp2(NB - 1)
            high_g(NB - 1)

        @block.vector
        def _(eng):
            ch = Count(eng, s_dv)
            eng.memset(zrow[:, :], 0.0).then_inc(s_zr, 1)
            eng.memset(gT[:, :, :], 0.0)
            eng.memset(tacc[:, :, :], 0.0)
            ch.link(eng.memset(qm[:, :, :], 0.0))
            for q in range(4):
                eng.memset(f4[32 * q:32 * q + 32, :], float(q))
                eng.memset(qm[32 * q:32 * q + 32, q, :], 1.0)
            ch.link(eng.memset(sm[:, :], 0.0))
            eng.wait_ge(d_small, 16)
            eng.wait_ge(s_cst, 1)
            eng.tensor_scalar(cidx[:, :], condi[:, :], float(P), pf[:, 0:1], ALU.mult, ALU.add).then_inc(s_cidx, 1)
            eng.wait_ge(d_gw, 16)
            for f in range(4):
                mm = eng.tensor_copy(gwp.rearrange("e (f j a) -> e f j a", f=4, j=8)[:, f],
                                     gw.rearrange("e (f a j) -> e f j a", f=4, j=8)[:, f])
            mm.then_inc(s_gwp, 1)
            eng.wait_ge(s_gt, 1)
            eng.tensor_copy(gT[:, :, 0:E], bank(4).rearrange("p (k e) -> p k e", k=8)).then_inc(s_gte, 1)
            eng.wait_ge(d_bc, 16 * 9)
            ch.link(eng.tensor_scalar(mkt[:, 0, :], adi[:, :], -float(R), pf[:, 0:1], ALU.mult, ALU.add))
            ch.link(eng.tensor_scalar(mkt[:, 1, :], mkt[:, 0, :], 0.0, scp[:, 0:1], ALU.is_ge, ALU.mult))
            eng.scalar_tensor_tensor(mk[:, :], mkt[:, 0, :], R - 0.5, mkt[:, 1, :], ALU.is_le, ALU.mult)

            def evac_t(i, f):
                eng.wait_ge(s_T, 2 * i + f + 1)
                if i >= 2:
                    eng.wait_ge(s_lg, i - 1)
                eng.tensor_copy(yT[:, i % 2, 4 * f:4 * f + 4, :], bank(2 + f)).then_inc(s_yT, 1)

            seen = {}

            def top(i):
                eng.wait_ge(s_lgc, i + 1)
                seen["m", i] = ch.mark(eng.max(m8[:, i % 4, :], lgs[:, i % 4, :]))

            def shift(i):
                eng.wait_ge(s_dv, seen["m", i])
                b = i % 4
                eng.tensor_scalar(z8[:, b, :], m8[:, b, :], m8[:, b, 0:1], ZMIN, ALU.subtract, ALU.max)
                eng.tensor_scalar(zz[:, b, :], lgs[:, b, :], m8[:, b, 0:1], ZMIN, ALU.subtract, ALU.max)\
                   .then_inc(s_z, 1)

            def choose(i):
                eng.wait_ge(s_z, i + 1)
                b = i % 4
                seen["r", i] = ch.mark(eng.match_replace(zr[:, b, :], z8[:, b, :], zz[:, b, :], 1.0))

            def marks(i):
                eng.wait_ge(s_dv, seen["r", i])
                b = i % 4
                if i >= 4:
                    eng.wait_ge(s_cum, i - 2)
                eng.tensor_scalar(mask[:, b, :], zr[:, b, :], 0.5, None, ALU.is_ge).then_inc(s_mask, 1)
                if i:
                    eng.wait_ge(s_mask, 2 * i)
                    eng.scalar_tensor_tensor(macc[:, b, :], zr[:, b, :], 0.5, macc[:, (i - 1) % 4, :],
                                             ALU.is_ge, ALU.add).then_inc(s_mask, 1)
                else:
                    eng.tensor_scalar(macc[:, 0, :], zr[:, 0, :], 0.5, None, ALU.is_ge).then_inc(s_mask, 1)

            def weigh(i):
                b = i % 4
                eng.wait_ge(s_e, i + 1)
                seen["w", i] = ch.mark(eng.scalar_tensor_tensor(
                    wm[:, b, :], zr[:, b, :], 0.5, eb[:, b, :], ALU.is_ge, ALU.mult, accum_out=sm[:, b:b + 1]))

            def invert(i):
                eng.wait_ge(s_dv, seen["w", i])
                b = i % 4
                seen["c", i] = ch.mark(eng.reciprocal(rc[:, b:b + 1], sm[:, b:b + 1]))

            def share(i):
                eng.wait_ge(s_dv, seen["c", i])
                b = i % 4
                eng.tensor_scalar(wy[:, i, :], wm[:, b, :], rc[:, b:b + 1], None, ALU.mult).then_inc(s_wy, 1)

            def tiles(i):
                eng.wait_ge(s_cte, i + 1)
                if i:
                    eng.wait_ge(s_cb, i)
                eng.scalar_tensor_tensor(tacc[:, 0, :], cb[:, i % 4, :], slot[:, 0:1], tacc[:, 0, :],
                                         ALU.is_le, ALU.add)
                eng.scalar_tensor_tensor(tacc[:, 1, :], cb[:, i % 4, :], slot[:, 1:2], tacc[:, 1, :],
                                         ALU.is_le, ALU.add).then_inc(s_cb, 1)

            for i in range(NB + 8):
                a = i - 3
                if 0 <= a < NB:
                    top(a)
                if 1 <= i <= NB:
                    evac_t(i - 1, 0)
                if 0 <= a < NB:
                    shift(a)
                if 0 <= i - 6 < NB:
                    tiles(i - 6)
                if 0 <= a - 1 < NB:
                    weigh(a - 1)
                if 0 <= a < NB:
                    choose(a)
                if 0 <= a - 1 < NB:
                    invert(a - 1)
                if 1 <= i <= NB:
                    evac_t(i - 1, 1)
                if 0 <= a < NB:
                    marks(a)
                if 0 <= a - 1 < NB:
                    share(a - 1)
            eng.wait_ge(s_cb, NB)
            eng.tensor_scalar(t128[:, :, :], tacc[:, :, :], float(P), None, ALU.mult)
            ch.link(eng.tensor_tensor(rowi[:, :].rearrange("p (c e) -> p c e", c=2), tacc[:, :, :], e32[:, :, :],
                                      ALU.add))
            eng.engine_nop().then_inc(s_idx, 1)

            def split(k, e):
                n = pos[(k, e)]
                eng.wait_ge(s_H, n + 1)
                eng.tensor_tensor(LR[:, n % NHL, :], raw[:, n % NRAW, :], HR[:, n % NHL, :].bitcast(F32),
                                  ALU.subtract).then_inc(s_L, 1)

            def turn_x(e, c):
                eng.wait_ge(d_xg[c], 64 * (e + 1))
                if e:
                    eng.wait_ge(s_vl, 2 * (e - 1) + c + 1)
                eng.transpose(XR[:, c, :, :, :].rearrange("p q j t -> p (q j t)"),
                              Xg[:, c, :, :].rearrange("p q s -> p (q s)")).then_inc(s_vt, 1)

            def low_x(e, c):
                eng.wait_ge(s_vh, 2 * e + c + 1)
                eng.tensor_tensor(XL[:, e % 2, c, :, :].rearrange("p j (q t) -> p q j t", q=4), XR[:, c, :, :, :],
                                  XH[:, e % 2, c, :, :].rearrange("p j (q t) -> p q j t", q=4).bitcast(F32),
                                  ALU.subtract).then_inc(s_vl, 1)

            def index(e):
                q = fq[("i", e)]
                eng.wait_ge(s_f, q + 1)
                eng.tensor_scalar(idx4[:, e % 4, :], bank(6 + q % 2, 0, 8), 4.0, f4[:, 0:1], ALU.mult, ALU.add)\
                   .then_inc(s_i4, 1)
                eng.wait_ge(s_i4, e + 1)
                eng.engine_nop().then_inc(s_fl, 1)

            def low_h(e, c):
                q = fq[("h", e, c)]
                eng.wait_ge(s_fh, 2 * e + c + 1)
                eng.tensor_tensor(hL[:, c, :, :].rearrange("p k n -> p (k n)"), bank(6 + q % 2, 0, I),
                                  hH[:, c, :, :].rearrange("p k n -> p (k n)").bitcast(F32),
                                  ALU.subtract).then_inc(s_fl, 1)

            def product(e, c):
                eng.wait_ge(s_sl, 2 * e + c + 1)
                if e:
                    eng.wait_ge(s_f, fq[("h", e - 1, c)] + 1)
                eng.tensor_tensor(prod[:, c, :, :].rearrange("q j p -> q p j"),
                                  sil[:, c, :].rearrange("q (p j) -> q p j", j=3),
                                  bank(2 * c + 1, 0, I).rearrange("q (p j) -> q p j", j=3),
                                  ALU.mult).then_inc(s_hp, 1)

            def token(e):
                eng.wait_ge(d_g[e % 2], 32 * (e // 2 + 1))
                for c in range(2):
                    ins = eng.tensor_scalar(Gj[:, c, :], G[:, e % 2, c, :], slot[:, c:c + 1], None,
                                            ALU.is_le, ALU.add, accum_out=cnt[:, c:c + 1])
                    n = ch.mark(ins)
                eng.wait_ge(s_dv, n)
                for c in range(2):
                    n = ch.mark(eng.tensor_scalar(tokf[:, e % 4, c:c + 1], t128[:, c, e:e + 1], cnt[:, c:c + 1],
                                                  dum[:, c:c + 1], ALU.add, ALU.min))
                eng.wait_ge(s_dv, n)
                eng.tensor_copy(toki[:, :].rearrange("p (c e) -> p c e", c=2)[:, :, e], tokf[:, e % 4, :])
                eng.tensor_tensor(tokq[:, e % 4, :].rearrange("p (q c) -> p q c", q=4), qm[:, :, :],
                                  tokf[:, e % 4, :].unsqueeze(1).to_broadcast([P, 4, 2]), ALU.mult)\
                   .then_inc(s_tok, 2)

            def column(e):
                eng.wait_ge(d_wg[e % 2], 32 * (e // 2 + 1))
                eng.tensor_copy(wcol[:, :].rearrange("p (c e) -> p c e", c=2)[:, :, e], Wg[:, e % 2, :, e])\
                   .then_inc(s_wc, 1)

            for k in ("gA", "uA", "gB"):
                split(k, 0)
            token(0)
            index(0)
            token(1)
            index(1)
            split("uB", 0)
            for c in range(2):
                turn_x(0, c)
            for c in range(2):
                low_x(0, c)
            for e in range(E + 1):
                if e >= 1:
                    low_h(e - 1, 0)
                    low_h(e - 1, 1)
                if e >= 1 and e + 2 < E:
                    index(e + 2)
                if e + 1 < E:
                    turn_x(e + 1, 0)
                    turn_x(e + 1, 1)
                    split("gA", e + 1)
                    low_x(e + 1, 0)
                    split("uA", e + 1)
                    low_x(e + 1, 1)
                    split("gB", e + 1)
                    split("uB", e + 1)
                    if e == 0:
                        column(0)
                    column(e + 1)
                if e == 0:
                    token(2)
                    index(2)
                if e < E:
                    product(e, 0)
                    product(e, 1)
                    split("dA", e)
                if e + 3 < E:
                    token(e + 3)
                if e < E:
                    split("dB", e)

            eng.wait_ge(d_sc, 32 * E)
            eng.wait_ge(s_bh, 1)
            eng.tensor_tensor(BL[:, :, D + NA:NX], laR[:, :, :, :].rearrange("p q a r -> p q (a r)"),
                              BH[:, :, D + NA:NX].bitcast(F32), ALU.subtract).then_inc(s_bl, 1)
            for n in range(17):
                eng.wait_ge(s_bh, n + 2)
                if n == 0:
                    ins = eng.tensor_tensor(BL[:, :, D:D + NA], bank(6, 0, 64).rearrange("p (q a) -> p q a", q=8),
                                            BH[:, :, D:D + NA].bitcast(F32), ALU.subtract)
                else:
                    j, f = divmod(n - 1, 2)
                    a = (slice(None), slice(4 * f, 4 * f + 4), slice(j * P, (j + 1) * P))
                    ins = eng.tensor_tensor(BL[a], bank(BF[n % 8]).rearrange("p (q n) -> p q n", q=4),
                                            BH[a].bitcast(F32), ALU.subtract)
                ins.then_inc(s_bl, 1)

            def low_w(k):
                eng.wait_ge(s_wh, k + 1)
                src = wr(k) if k < 8 else bmR[:, :, :, :].rearrange("p q a r -> p q (a r)")
                eng.tensor_tensor(WL[:, k % 2, :, :], src, WH[:, k % 2, :, :].bitcast(F32), ALU.subtract)\
                   .then_inc(s_wl, 1)

            def low_m(k):
                eng.wait_ge(s_mh, k + 1)
                b0 = 3 * (k % 2)
                eng.tensor_tensor(ML[:, k, 0:768].rearrange("p (g n) -> p g n", g=2), ps[:, b0:b0 + 2, 0:384],
                                  MH[:, k, 0:768].rearrange("p (g n) -> p g n", g=2).bitcast(F32), ALU.subtract)
                eng.tensor_tensor(ML[:, k, 768:NX], bank(b0 + 2, 0, NX - 768), MH[:, k, 768:NX].bitcast(F32),
                                  ALU.subtract).then_inc(s_ml, 1)

            low_w(0)
            low_w(1)
            for k in range(9):
                low_m(k)
                if k + 2 < 9:
                    low_w(k + 2)

            eng.wait_ge(s_lbh, 1)
            eng.tensor_tensor(lbL[:, :], lb, lbH[:, :].bitcast(F32), ALU.subtract).then_inc(s_lbl, 1)
            eng.memset(z2[:, 8:14], 1e30).then_inc(s_pad, 1)
            for f in range(2):
                eng.wait_ge(s_ath, f + 1)
                eng.tensor_tensor(ATL[:, 4 * f:4 * f + 4, :].rearrange("p k n -> p (k n)"), bank(6 + f),
                                  ATH[:, 4 * f:4 * f + 4, :].rearrange("p k n -> p (k n)").bitcast(F32),
                                  ALU.subtract).then_inc(s_atl, 1)

            def low_t(t, f):
                eng.wait_ge(s_xh, 2 * t + f + 1)
                g, o = t // 2, (t % 2) * P
                a = (slice(None), g % 2, slice(4 * f, 4 * f + 4), slice(o, o + P))
                eng.tensor_tensor(xTL[a], bank(6).rearrange("p (k n) -> p k n", k=4), xTH[a].bitcast(F32),
                                  ALU.subtract).then_inc(s_xl, 1)

            def low_a(g):
                for o in range(2):
                    b = 2 * g + o
                    eng.wait_ge(s_xah, 2 * g + 2)
                    a = (slice(None), g % 2, slice(o * P, (o + 1) * P))
                    eng.scalar_tensor_tensor(xaL[a], bank(7, o * P, (o + 1) * P), mk[:, b:b + 1], xaH[a].bitcast(F32),
                                             ALU.mult, ALU.subtract).then_inc(s_xal, 1)

            def gate_of(t):
                b2 = 3 * (t % 2) + 2
                eng.wait_ge(s_mm, t + 1)
                if t == 0:
                    eng.wait_ge(d_bi, 32)
                    eng.wait_ge(s_pad, 1)
                ch.link(eng.tensor_tensor(lg2[:, :], bank(b2, 256, 264), rb[:, :], ALU.add))
                ch.link(eng.tensor_reduce(mx2[:, :], lg2[:, :], AX_X, ALU.max))
                if t:
                    eng.wait_ge(s_e2, t)
                ch.link(eng.tensor_scalar(z2[:, 0:NA], lg2[:, :], mx2[:, 0:1], ZMIN, ALU.subtract, ALU.max))
                eng.engine_nop().then_inc(s_z2, 1)
                ch.link(eng.max(t8[:, :], z2[:, :]))
                ch.link(eng.match_replace(zr2[:, :], t8[:, :], z2[:, :], 1.0))
                eng.wait_ge(s_e2, t + 1)
                ch.link(eng.scalar_tensor_tensor(g2[:, :], zr2[:, 0:NA], 0.5, e2[:, t % 2, :], ALU.is_ge, ALU.mult,
                                                 accum_out=sm2[:, 0:1]))
                ch.link(eng.reciprocal(sm2[:, 1:2], sm2[:, 0:1]))
                ch.link(eng.tensor_scalar(gate[:, :], g2[:, :], sm2[:, 1:2], 2.0, ALU.mult, ALU.mult))
                if t:
                    eng.wait_ge(s_mt, t)
                eng.tensor_tensor(mg[:, :].rearrange("p (a r) -> p a r", a=NA),
                                  bank(b2, 264, 392).rearrange("p (a r) -> p a r", a=NA),
                                  gate[:, :].unsqueeze(2).to_broadcast([P, NA, R]), ALU.mult).then_inc(s_mg, 1)

            def low_g(t):
                eng.wait_ge(s_mth, t + 1)
                eng.tensor_tensor(mgL[:, :], bank(7, 256, 384), mgH[:, :].bitcast(F32), ALU.subtract)\
                   .then_inc(s_mtl, 1)

            def final(t):
                b0, s = 3 * (t % 2), t % 6
                eng.wait_ge(s_lo, t + 1)
                eng.wait_ge(s_pb, t + 1)
                if t >= 3:
                    eng.wait_ge(d_o[t % 3], 16 * (t // 3))
                eng.tensor_tensor(osb[:, t % 3, 0:768].rearrange("p (g n) -> p g n", g=2), ps[:, b0:b0 + 2, 0:384],
                                  x1[:, s, 0:768].rearrange("p (g n) -> p g n", g=2), ALU.add).then_inc(s_fin, 1)
                eng.tensor_tensor(osb[:, t % 3, 768:D], bank(b0 + 2, 0, 256), x1[:, s, 768:D],
                                  ALU.add).then_inc(s_fin, 1)

            for t in range(2):
                for f in range(2):
                    low_t(t, f)
            low_a(0)
            for t in range(NB):
                if t:
                    gate_of(t - 1)
                if t + 2 < NB:
                    low_t(t + 2, 0)
                if t:
                    low_g(t - 1)
                if t + 2 < NB:
                    low_t(t + 2, 1)
                if t:
                    final(t - 1)
                if t % 2 and t + 1 < NB:
                    low_a(t // 2 + 1)
            gate_of(NB - 1)
            low_g(NB - 1)
            final(NB - 1)


_INS = ["x", "itok_B_1_198", "itok_B_0_6", "L0_cond_weights", "L0_ffn_gate_w", "L0_ffn_wg", "L0_ffn_wu", "L0_ffn_wd",
        "L1_cond_W", "L1_cond_A", "L1_cond_Bm", "L1_cond_scalings", "L1_ffn_base_w", "L1_ffn_base_b",
        "L1_ffn_router_w", "L1_ffn_router_b", "L1_ffn_lora_A", "L1_ffn_lora_B"]


def kernel(**inputs):
    import numpy as _np
    import concourse.bacc as _bacc
    from concourse import mybir as _mybir
    from concourse.bass_utils import run_bass_kernel_spmd as _run

    nc = _bacc.Bacc("TRN2", target_bir_lowering=False, num_devices=1)
    arrays, args = {}, []
    for name in _INS:
        a = _np.ascontiguousarray(inputs[name])
        arrays[f"in_{name}"] = a
        args.append(nc.dram_tensor(f"in_{name}", a.shape, _mybir.dt.from_np(a.dtype), kind="ExternalInput").ap())
    o = nc.dram_tensor("out_0", (32, 128, 1024), _mybir.dt.float32, kind="ExternalOutput").ap()
    adaln_ffn_kernel(nc, *args, o)
    r = _run(nc, [arrays], core_ids=[0])
    return r.results[0]["out_0"]
```

```python
from contextlib import ExitStack

import concourse.bass as bass
from concourse import mybir

F32 = mybir.dt.float32
F32R = mybir.dt.float32r
BF16 = mybir.dt.bfloat16
I32 = mybir.dt.int32
ALU = mybir.AluOpType
ACT = mybir.ActivationFunctionType
AX_X = mybir.AxisListType.X

P = 128
NB = 32
D = 1024
E = 64
I = 384
CAP = 256
TOK = NB * P
NA = 8
R = 16
NX = D + NA + NA * R
CG = [(0, 384), (384, 768), (768, NX)]
UN = 1536
NRAW = 4
NHL = 8
NY = 4
NS = 3
FILL = 4
NB0 = 9
ZMIN = -87.8


class Count:

    def __init__(self, eng, sem):
        self.eng, self.sem, self.n = eng, sem, 0

    def mark(self, ins):
        self.n += 1
        ins.then_inc(self.sem, 1)
        return self.n

    def link(self, ins):
        self.eng.wait_ge(self.sem, self.mark(ins))


def adaln_ffn_kernel(nc, x, cond, adap, w0, gate_w, wg, wu, wd, W, A, Bm, scal,
                     base_w, base_b, router_w, router_b, lora_A, lora_B, out):
    x_r = x.rearrange("b c t -> (b c) t")
    out_r = out.rearrange("b c t -> (b c) t")
    w0_r = w0.rearrange("s c d -> (s c) d")
    yd = nc.dram_tensor("yd", (TOK + 2 * P, D), F32, kind="Internal").ap()
    yd4 = yd.rearrange("t (f s) -> (t f) s", f=4)
    wdr = nc.dram_tensor("wdr", (TOK + 2 * P, E), F32, kind="Internal").ap()
    acc = nc.dram_tensor("accd", (TOK + 2 * P, D), F32, kind="Internal").ap()
    tab = nc.dram_tensor("tabd", (E * NB + 1, P), F32, kind="Internal").ap()
    tab_v = tab[0:E * NB, :].rearrange("(e i) t -> i e t", i=NB)

    with ExitStack() as ctx:
        def sb(name, shape, dt, stack=None):
            return (stack or ctx).enter_context(nc.sbuf_tensor(name, shape, dt))

        def sem(name):
            return ctx.enter_context(nc.semaphore(name))

        ps = ctx.enter_context(nc.psum_tensor("ps", [P, 8, 512], F32))

        def bank(b, a=0, z=512, p=P):
            return ps[0:p, b, a:z]

        ident = sb("ident", [P, P], F32)
        tri = sb("tri", [P, P], BF16)
        ones = sb("ones", [P, P], BF16)
        slot = sb("slot", [P, 2], F32)
        dum = sb("dum", [P, 2], F32)
        pf = sb("pf", [P, 1], F32)
        t128 = sb("t128", [P, 2, E], F32)
        rowi = sb("rowi", [P, 2 * E], I32)
        toki = sb("toki", [P, 2 * E], I32)
        wcol = sb("wcol", [P, 2 * E], F32)
        mk = sb("mk", [P, NB], F32)
        f4 = sb("f4", [P, 1], F32)
        rep = sb("rep", [P, P], F32)
        qm = sb("qm", [P, 4, 2], F32)
        laR = sb("laR", [P, 8, NA, R], F32)
        bmR = sb("bmR", [P, 8, NA, R], F32)

        moe = ExitStack()
        raw = sb("raw", [P, NRAW, UN], F32, moe)
        rt0 = ExitStack()
        wall = sb("wall", [P, 16, P], F32, rt0)
        yrow = sb("yrow", [P, NY, D], F32, rt0)
        rt0.close()
        hH = sb("hH", [P, 2, 3, P], F32R, moe)
        hL = sb("hL", [P, 2, 3, P], F32R, moe)
        ot = sb("ot", [P, 2, D], F32, moe)
        Wg = sb("Wg", [P, 2, 2, E], F32, moe)
        tokf = sb("tokf", [P, 4, 2], F32, moe)
        tokq = sb("tokq", [P, 4, 8], F32, moe)
        idx4 = sb("idx4", [P, 4, 8], I32, moe)
        sil = sb("sil", [P, 2, I], F32, moe)
        prod = sb("prod", [P, 2, 3, P], F32, moe)
        G = sb("G", [P, 2, 2, P], F32, moe)
        Gj = sb("Gj", [P, 2, P], F32, moe)
        cnt = sb("cnt", [P, 2], F32, moe)
        HR = sb("HR", [P, NHL, UN], F32R, moe)
        LR = sb("LR", [P, NHL, UN], F32R, moe)

        rt = ExitStack()
        xt = sb("xt", [P, 4, D], F32, rt)
        wy = sb("wy", [P, NB, E], F32, rt)
        yT = sb("yT", [P, 2, 8, P], F32, rt)
        gT = sb("gT", [P, 8, P], F32, rt)
        gw = raw[0:E, 0, 0:D]
        gwp = raw[0:E, 1, 0:D]
        zrow = sb("zrow", [P, 256], F32, rt)
        e32 = sb("e32", [P, 2, E], F32, rt)
        tacc = sb("tacc", [P, 2, E], F32, rt)
        condi = sb("condi", [P, NB], I32, rt)
        adi = sb("adi", [P, NB], I32, rt)
        cidx = sb("cidx", [P, NB], I32, rt)
        scp = sb("scp", [P, 1], F32, rt)
        mkt = sb("mkt", [P, 3, NB], F32, rt)
        lgs = sb("lgs", [P, 4, E], F32, rt)
        m8 = sb("m8", [P, 4, 8], F32, rt)
        z8 = sb("z8", [P, 4, 8], F32, rt)
        zz = sb("zz", [P, 4, E], F32, rt)
        zr = sb("zr", [P, 4, E], F32, rt)
        eb = sb("eb", [P, 4, E], F32, rt)
        wm = sb("wm", [P, 4, E], F32, rt)
        sm = sb("sm", [P, 4], F32, rt)
        rc = sb("rc", [P, 4], F32, rt)
        mask = sb("mask", [P, 4, E], BF16, rt)
        macc = sb("macc", [P, 4, E], BF16, rt)
        ct = sb("ct", [E, 4, P], F32, rt)
        cb = sb("cb", [P, 4, E], F32, rt)
        rt.close()

        Xg = sb("Xg", [P, 2, 4, 256], F32, moe)
        XR = sb("XR", [P, 2, 4, 8, 32], F32, moe)
        XH = sb("XH", [P, 2, 2, 8, P], F32R, moe)
        XL = sb("XL", [P, 2, 2, 8, P], F32R, moe)
        moe.close()

        x1 = sb("x1", [P, 6, D], F32)
        MH = sb("MH", [P, 9, NX], F32R)
        ML = sb("ML", [P, 9, NX], F32R)
        pre = ExitStack()
        WL = sb("WL", [P, 2, 8, P], F32R, pre)
        WH = sb("WH", [P, 2, 8, P], F32R, pre)
        BH = sb("BH", [P, 8, NX], F32R, pre)
        BL = sb("BL", [P, 8, NX], F32R, pre)
        pre.close()
        ar, lb, arp = x1[:, 4, :], x1[:, 5, :], x1[:, 3, :]

        def xq(t):
            return (bmR if t % 2 else laR)[:, :, :, :].rearrange("p q a r -> p (q a r)")

        def wr(k):
            return x1[:, 2 + k % 2, :].rearrange("p (q d) -> p q d", q=8)

        xTH = sb("xTH", [P, 2, 8, 2 * P], F32R)
        xTL = sb("xTL", [P, 2, 8, 2 * P], F32R)
        ATH = sb("ATH", [P, 8, P], F32R)
        ATL = sb("ATL", [P, 8, P], F32R)
        lbH = sb("lbH", [P, D], F32R)
        lbL = sb("lbL", [P, D], F32R)
        bias = sb("bias", [P, D], F32)
        rb = sb("rb", [P, NA], F32)
        xaH = sb("xaH", [P, 2, 2 * P], F32R)
        xaL = sb("xaL", [P, 2, 2 * P], F32R)
        lg2 = sb("lg2", [P, NA], F32)
        xr = sb("xr", [P, 2, 4, 8, 32], F32)
        mx2 = sb("mx2", [P, 1], F32)
        z2 = sb("z2", [P, 14], F32)
        t8 = sb("t8", [P, 8], F32)
        zr2 = sb("zr2", [P, 14], F32)
        e2 = sb("e2", [P, 2, NA], F32)
        g2 = sb("g2", [P, NA], F32)
        sm2 = sb("sm2", [P, 2], F32)
        gate = sb("gate", [P, NA], F32)
        mg = sb("mg", [P, P], F32)
        mgH = sb("mgH", [P, P], F32R)
        mgL = sb("mgL", [P, P], F32R)
        osb = sb("osb", [P, 3, D], F32)

        d_small, d_bc, d_gw, d_la = sem("d_small"), sem("d_bc"), sem("d_gw"), sem("d_la")
        d_z = sem("d_z")
        d_ad = [sem(f"d_ad{i}") for i in range(2)]
        d_x = [sem(f"d_x{i}") for i in range(4)]
        d_as = [sem(f"d_as{i}") for i in range(4)]
        d_ys = [sem(f"d_ys{i}") for i in range(NY)]
        d_ts = [sem(f"d_ts{i}") for i in range(4)]
        d_wy = sem("d_wy")
        s_lgc = sem("s_lgc")
        d_w = [sem(f"d_w{i}") for i in range(8)]
        WG = [(b, b + 1) for b in range(4)] + [(b, b + 7) for b in range(4, NB, 7)]
        wgroup = {b: g for g, (lo, hi) in enumerate(WG) for b in range(lo, hi)}
        s_pc, s_cst, s_cidx, s_dv, s_zr = sem("s_pc"), sem("s_cst"), sem("s_cidx"), sem("s_dv"), sem("s_zr")
        s_gt, s_gte = sem("s_gt"), sem("s_gte")
        s_Y, s_yr, s_T, s_yT, s_lg = sem("s_Y"), sem("s_yr"), sem("s_T"), sem("s_yT"), sem("s_lg")
        s_z, s_e, s_wy, s_mask, s_cum = sem("s_z"), sem("s_e"), sem("s_wy"), sem("s_mask"), sem("s_cum")
        s_cte, s_cb, s_idx = sem("s_cte"), sem("s_cb"), sem("s_idx")
        d_raw = [sem(f"d_raw{i}") for i in range(NRAW)]
        s_H, s_L, s_k, s_dn = sem("s_H"), sem("s_L"), sem("s_k"), sem("s_dn")
        s_f, s_fh, s_fl = sem("s_f"), sem("s_fh"), sem("s_fl")
        s_sl, s_hp, s_out, s_tok, s_wc = sem("s_sl"), sem("s_hp"), sem("s_out"), sem("s_tok"), sem("s_wc")
        d_g = [sem(f"d_g{i}") for i in range(2)]
        d_xg = [sem(f"d_xg{i}") for i in range(2)]
        d_wg = [sem(f"d_wg{i}") for i in range(2)]
        s_vt, s_vh, s_vl, s_i4, s_gwp = sem("s_vt"), sem("s_vh"), sem("s_vl"), sem("s_i4"), sem("s_gwp")
        d_sc = sem("d_sc")
        d_bw = [sem(f"d_bw{i}") for i in range(5)]
        d_wr = [sem(f"d_wr{i}") for i in range(2)]
        s_bf, s_bh, s_bl, s_wh, s_wl = sem("s_bf"), sem("s_bh"), sem("s_bl"), sem("s_wh"), sem("s_wl")
        s_m, s_mh, s_ml = sem("s_m"), sem("s_mh"), sem("s_ml")
        d_ab, d_bi = sem("d_ab"), sem("d_bi")
        d_x1 = [sem(f"d_x1{i}") for i in range(6)]
        d_xq = [sem(f"d_xq{i}") for i in range(2)]
        s_xr, s_arp = sem("s_xr"), sem("s_arp")
        d_o = [sem(f"d_o{i}") for i in range(3)]
        s_at, s_ath, s_atl, s_lbh, s_lbl = sem("s_at"), sem("s_ath"), sem("s_atl"), sem("s_lbh"), sem("s_lbl")
        s_xh, s_xl = sem("s_xh"), sem("s_xl")
        s_xa, s_xah, s_xal = sem("s_xa"), sem("s_xah"), sem("s_xal")
        s_mm, s_z2, s_e2, s_mg, s_mt, s_mth, s_mtl = [sem(n) for n in ("s_mm", "s_z2", "s_e2", "s_mg", "s_mt", "s_mth", "s_mtl")]
        s_lo, s_fin, s_pb, s_pad = sem("s_lo"), sem("s_fin"), sem("s_pb"), sem("s_pad")

        units, pos = [], {}

        def stream(kinds, e):
            for k in kinds:
                pos[(k, e)] = len(units)
                units.append((k, e))

        stream(["gA", "uA", "gB", "uB"], 0)
        for e in range(1, E):
            stream(["gA", "uA", "gB", "uB"], e)
            stream(["dA", "dB"], e - 1)
        stream(["dA", "dB"], E - 1)

        def unit_src(n):
            k, e = units[n]
            h = 0 if k[1] == "A" else UN
            if k[0] == "d":
                v = wd[e].rearrange("(p j) h -> p (j h)", j=3)
            else:
                v = (wg if k[0] == "g" else wu)[e].rearrange("(p k) i -> p (k i)", k=8)
            return v[:, h:h + UN]

        def wait_retired(eng, n):
            k, e = units[n]
            if k[0] == "d":
                eng.wait_ge(s_dn, 4 * (e + 1))
            else:
                eng.wait_ge(s_k, 2 * e + (1 if k[1] == "A" else 2))

        SB = [0, 1, 4, 5]

        fq = {}
        for e in range(2):
            fq[("i", e)] = len(fq)
        for e in range(E):
            if e + 2 < E:
                fq[("i", e + 2)] = len(fq)
            for c in range(2):
                fq[("h", e, c)] = len(fq)

        def bcast(ap1, n):
            return ap1.rearrange("(a n) -> a n", a=1).to_broadcast([P, n])

        block = ctx.enter_context(nc.Block())

        @block.sync
        def _(eng):
            eng.dma_start(condi[:, :], bcast(cond, NB)).then_inc(d_small, 16)
            eng.dma_start(gw, gate_w).then_inc(d_gw, 16)
            eng.dma_start(adi[:, :], bcast(adap, NB)).then_inc(d_bc, 16)
            for a in range(NA):
                eng.dma_start(scp[R * a:R * a + R, :],
                              scal[a:a + 1].rearrange("(a n) -> a n", a=1).to_broadcast([R, 1])).then_inc(d_bc, 16)

            def load_unit(n):
                if n >= NRAW:
                    eng.wait_ge(s_L, n - NRAW + 1)
                eng.dma_start(raw[:, n % NRAW, :], unit_src(n)).then_inc(d_raw[n % NRAW], 16)

            for i in range(NB + 1):
                if i < NB:
                    if i >= 4:
                        eng.wait_ge(s_Y, 2 * (i - 3))
                        if i % 4 < NS:
                            eng.wait_ge(d_as[i % 4], 16 * (i // 4))
                    eng.dma_start(xt[:, i % 4, :], x_r[i * P:(i + 1) * P, :]).then_inc(d_x[i % 4], 16)
                if i == 20:
                    eng.wait_ge(s_zr, 1)
                    for c in range(2):
                        r0 = TOK + c * P
                        for q in range(4):
                            eng.dma_start(yd[r0:r0 + P, q * 256:(q + 1) * 256], zrow[:, :]).then_inc(d_z, 16)
                            eng.dma_start(acc[r0:r0 + P, q * 256:(q + 1) * 256], zrow[:, 0:256]).then_inc(d_z, 16)
                        eng.dma_start(wdr[r0:r0 + P, :], zrow[:, 0:E]).then_inc(d_z, 16)
                    eng.dma_start(tab[E * NB:E * NB + 1, :], zrow[0:1, 0:P]).then_inc(d_z, 16)
                if i >= 1 and (i - 1) % 4 < NS:
                    j = i - 1
                    eng.wait_ge(d_x[j % 4], 16 * (j // 4 + 1))
                    eng.dma_start(acc[j * P:(j + 1) * P, :], xt[:, j % 4, :]).then_inc(d_as[j % 4], 16)
            rest = [i for i in range(NB) if i % 4 >= NS]

            def fill(n):
                i = rest[n]
                if n >= 2:
                    eng.wait_ge(d_ad[n % 2], 16 * (n // 2))
                eng.dma_start(acc[i * P:(i + 1) * P, :], x_r[i * P:(i + 1) * P, :]).then_inc(d_ad[n % 2], 16)

            for n in range(len(units)):
                if n < NRAW:
                    i = NB - NRAW + n
                    eng.wait_ge(d_ys[i % NY], 16 * (i // NY + 1))
                load_unit(n)
                if n == 7:
                    for k in range(FILL):
                        fill(k)
                if n >= 8 and n - 8 + FILL < len(rest):
                    fill(n - 8 + FILL)
                if n >= 100 and n % 4 == 0 and n < 100 + 4 * NA:
                    e = (n - 100) // 4
                    with nc.allow_non_contiguous_dma(reason="64-byte rows"):
                        eng.dma_start(laR[:, :, e, :],
                                      lora_A[e].rearrange("(q p) r -> p q r", p=P)).then_inc(d_la, 16)
                        eng.dma_start(bmR[:, :, e, :],
                                      Bm[e].rearrange("(q p) r -> p q r", p=P)).then_inc(d_la, 16)

            def load_w(k):
                with nc.allow_non_contiguous_dma(reason="128-byte runs"):
                    for f in range(4):
                        c = f * 256 + 32 * k
                        eng.dma_start(wr(k)[:, :, 32 * f:32 * f + 32],
                                      W.rearrange("(q p) d -> p q d", p=P)[:, :, c:c + 32]).then_inc(d_wr[k % 2], 16)

            def load_b(j):
                if j >= 4:
                    eng.wait_ge(s_bf, 2 * j - 5)
                eng.dma_start(x1[:, SB[j % 4], :], base_w[j * P:(j + 1) * P, :]).then_inc(d_bw[j % 4], 16)

            eng.wait_ge(s_L, len(units) - 2)
            eng.dma_start(x1[0:NA, 2, :], router_w).then_inc(d_bw[4], 16)
            load_b(0)
            load_b(1)
            eng.wait_ge(s_L, len(units))
            load_b(2)
            load_b(3)
            load_w(1)
            eng.wait_ge(s_bf, 1)
            load_w(0)
            for j in range(4, 8):
                load_b(j)
            eng.wait_ge(s_bf, 17)
            eng.dma_start(ar, A.rearrange("a r d -> (a r) d")).then_inc(d_ab, 16)
            eng.dma_start(lb, lora_B.rearrange("e r d -> (e r) d")).then_inc(d_ab, 16)
            for k in range(2, 8):
                eng.wait_ge(s_wl, k - 1)
                load_w(k)

            def load_x(t):
                eng.dma_start(x1[:, t % 6, :], acc[t * P:(t + 1) * P, :]).then_inc(d_x1[t % 6], 16)

            eng.wait_ge(d_sc, 32 * E)
            eng.wait_ge(s_bf, 17)
            load_x(0)
            load_x(1)
            eng.wait_ge(s_wl, 8)
            load_x(2)

            def load_q(t):
                if t >= 2:
                    eng.wait_ge(s_xr, t - 1)
                for f in range(4):
                    eng.dma_start(xq(t)[32 * f:32 * f + 32, :].rearrange("s (q c) -> s q c", q=4),
                                  acc[t * P:(t + 1) * P, f * 256:(f + 1) * 256].rearrange("(q s) c -> s q c", q=4))\
                       .then_inc(d_xq[t % 2], 16)

            load_q(0)
            eng.wait_ge(s_wl, 9)
            load_q(1)
            eng.wait_ge(s_m, 9)
            eng.dma_start(bias[:, :], bcast(base_b, D)).then_inc(d_bi, 16)
            eng.dma_start(rb[:, :], bcast(router_b, NA)).then_inc(d_bi, 16)

            eng.wait_ge(s_at, 2)
            load_x(3)
            load_q(2)
            load_q(3)
            load_q(4)
            eng.wait_ge(s_lbl, 1)
            for t in range(4, NB + 6):
                if t >= 6:
                    eng.wait_ge(s_fin, 2 * (t - 5))
                    eng.dma_start(out_r[(t - 6) * P:(t - 5) * P, :], osb[:, t % 3, :]).then_inc(d_o[t % 3], 16)
                if t < NB:
                    eng.dma_start(x1[:, t % 6, :], acc[t * P:(t + 1) * P, :]).then_inc(d_x1[t % 6], 16)
                if 6 <= t < NB + 1:
                    load_q(t - 1)
            for s in range(3):
                eng.wait_ge(d_o[s], 16 * len(range(s, NB, 3)))

        @block.gpsimd
        def _(eng):
            ch = Count(eng, s_pc)
            eng.memset(ident[:, :], 0.0)
            eng.memset(ones[:, :], 1.0)
            eng.memset(rep[:, :], 0.0)
            ch.link(eng.memset(tri[:, :], 1.0))
            eng.affine_select(out=ident[:, :], in_=ident[:, :], compare_op=ALU.not_equal, fill=1.0,
                              base=0, pattern=[[-1, P]], channel_multiplier=1)
            eng.affine_select(out=tri[:, :], in_=tri[:, :], compare_op=ALU.is_ge, fill=0.0,
                              base=0, pattern=[[1, P]], channel_multiplier=-1)
            v = rep[:, :].rearrange("p (f t) -> p f t", f=4)
            for q in range(4):
                ch.link(eng.affine_select(out=v, in_=v, compare_op=ALU.not_equal, fill=1.0,
                                          base=-32 * q, pattern=[[0, 4], [-1, 32]], channel_multiplier=1))
            eng.iota(pf[:, :], [[0, 1]], base=0, channel_multiplier=1, allow_small_or_imprecise_dtypes=True)
            eng.iota(slot[:, :], [[P, 2]], base=0, channel_multiplier=1, allow_small_or_imprecise_dtypes=True)
            eng.iota(dum[:, :], [[P, 2]], base=TOK, channel_multiplier=1, allow_small_or_imprecise_dtypes=True)
            eng.iota(e32[:, :, :], [[0, 2], [NB, E]], base=0, channel_multiplier=0,
                     allow_small_or_imprecise_dtypes=True).then_inc(s_cst, 1)
            eng.wait_ge(s_cidx, 1)
            for b in range(NB):
                if b >= 16:
                    eng.wait_ge(s_Y, 2 * (b - 15))
                eng.indirect_dma_start(wall[:, b % 16, :], None, w0_r,
                                       bass.IndirectOffsetOnAxis(ap=cidx[:, b:b + 1], axis=0))\
                   .then_inc(d_w[wgroup[b]], 16)

            def gather_tab(e):
                if e == 0:
                    for s in range(4):
                        eng.wait_ge(d_ts[s], 16 * (NB // 4))
                    eng.wait_ge(d_z, 16 * 19)
                    eng.wait_ge(s_idx, 1)
                if e >= 2:
                    eng.wait_ge(s_tok, 2 * (e - 1))
                for c in range(2):
                    eng.indirect_dma_start(G[:, e % 2, c, :], None, tab,
                                           bass.IndirectOffsetOnAxis(ap=rowi[:, c * E + e:c * E + e + 1], axis=0))\
                       .then_inc(d_g[e % 2], 16)

            def gather_x(e):
                eng.wait_ge(s_i4, e + 1)
                if e == 0:
                    eng.wait_ge(d_wy, 16 * NB // 4)
                    for s in range(NY):
                        eng.wait_ge(d_ys[s], 16 * len(range(s, NB, NY)))
                    for s in range(NS):
                        eng.wait_ge(d_as[s], 16 * (NB // 4))
                for c in range(2):
                    if e:
                        eng.wait_ge(s_vt, 2 * (e - 1) + c + 1)
                    for q in range(4):
                        i = 2 * q + c
                        eng.indirect_dma_start(Xg[:, c, q, :], None, yd4,
                                               bass.IndirectOffsetOnAxis(ap=idx4[:, e % 4, i:i + 1], axis=0))\
                           .then_inc(d_xg[c], 16)

            def gather_w(e):
                if e >= 2:
                    eng.wait_ge(s_wc, e - 1)
                else:
                    eng.wait_ge(d_wy, 16 * NB // 4)
                for c in range(2):
                    eng.indirect_dma_start(Wg[:, e % 2, c, :], None, wdr,
                                           bass.IndirectOffsetOnAxis(ap=toki[:, c * E + e:c * E + e + 1], axis=0))\
                       .then_inc(d_wg[e % 2], 16)

            def scatter(e):
                if e >= 1:
                    eng.wait_ge(d_sc, 32 * e)
                else:
                    for s in range(2):
                        eng.wait_ge(d_ad[s], 16 * ((4 - NS) * (NB // 4) // 2))
                for c in range(2):
                    eng.wait_ge(s_out, 4 * e + 2 * c + 2)
                    eng.indirect_dma_start(acc, bass.IndirectOffsetOnAxis(ap=toki[:, c * E + e:c * E + e + 1], axis=0),
                                           ot[:, c, :], None, compute_op=ALU.add).then_inc(d_sc, 16)

            gather_tab(0)
            gather_tab(1)
            gather_x(0)
            gather_x(1)
            gather_tab(2)
            gather_w(0)
            gather_w(1)
            for e in range(E + 1):
                if e + 3 < E:
                    gather_tab(e + 3)
                if e + 2 < E:
                    gather_x(e + 2)
                    gather_w(e + 2)
                if e >= 1:
                    scatter(e - 1)
            eng.wait_ge(d_sc, 32 * E)

            eng.wait_ge(d_bi, 32)
            for t in range(NB):
                eng.wait_ge(d_x1[t % 6], 16 * (t // 6 + 1))
                eng.tensor_tensor(x1[:, t % 6, :], x1[:, t % 6, :], bias[:, :], ALU.add).then_inc(s_pb, 1)

        @block.tensor
        def _(eng):
            eng.wait_ge(s_cst, 1)
            eng.wait_ge(s_gwp, 1)
            for k in range(8):
                mm = eng.transpose(bank(4, k * E, (k + 1) * E), gwp[:, k * P:(k + 1) * P], ident[0:E, 0:E])
            mm.then_inc(s_gt, 1)

            def condition(i):
                g = wgroup[i]
                eng.wait_ge(d_w[g], 16 * (WG[g][1] - WG[g][0]))
                eng.wait_ge(d_x[i % 4], 16 * (i // 4 + 1))
                for h in range(2):
                    if i:
                        eng.wait_ge(s_yr, 2 * i - 1 + h)
                    eng.matmul(bank(h), wall[:, i % 16, :], xt[:, i % 4, h * 512:(h + 1) * 512],
                               start=True, stop=True).then_inc(s_Y, 1)

            def turn(i):
                eng.wait_ge(s_yr, 2 * i + 2)
                for f in range(2):
                    n = 2 * i + f
                    if n >= 2:
                        eng.wait_ge(s_yT, n - 1)
                    for q in range(4):
                        k = 4 * f + q
                        mm = eng.transpose(bank(2 + f, q * P, (q + 1) * P), yrow[:, i % NY, k * P:(k + 1) * P],
                                           ident[:, :])
                    mm.then_inc(s_T, 1)

            def logits(i):
                if i == 0:
                    eng.wait_ge(s_gte, 1)
                eng.wait_ge(s_yT, 2 * i + 2)
                if i >= 2:
                    eng.wait_ge(s_lgc, i - 1)
                for k in range(8):
                    mm = eng.matmul(bank(4 + i % 2, 0, E), yT[:, i % 2, k, :], gT[:, k, 0:E], start=(k == 0), stop=(k == 7))
                mm.then_inc(s_lg, 1)

            def counts(i):
                eng.wait_ge(s_mask, 2 * i + 2)
                if i >= 2:
                    eng.wait_ge(s_cte, i - 1)
                b = 6 + i % 2
                eng.matmul(bank(b, 0, P, E), mask[:, i % 4, :], tri[:, :], start=True, stop=(i == 0))
                if i:
                    eng.matmul(bank(b, 0, P, E), macc[:, (i - 1) % 4, :], ones[:, :], start=False, stop=True)
                eng.matmul(bank(b, P, P + E), ones[:, :], macc[:, i % 4, :], start=True, stop=True)\
                   .then_inc(s_cum, 1)

            for i in range(NB + 4):
                if i < NB:
                    condition(i)
                if 1 <= i <= NB:
                    turn(i - 1)
                if 2 <= i <= NB + 1:
                    logits(i - 2)
                if i >= 4:
                    counts(i - 4)

            def repeat(e):
                q = fq[("i", e)]
                if q >= 2:
                    eng.wait_ge(s_fl, q - 1)
                else:
                    eng.wait_ge(s_cte, NB)
                eng.wait_ge(s_tok, 2 * e + 2)
                eng.matmul(bank(6 + q % 2, 0, 8), rep[:, :], tokq[:, e % 4, :], start=True, stop=True)\
                   .then_inc(s_f, 1)

            def turn_h(e, c):
                q = fq[("h", e, c)]
                eng.wait_ge(s_fl, q - 1)
                eng.wait_ge(s_hp, 2 * e + c + 1)
                for j in range(3):
                    mm = eng.transpose(bank(6 + q % 2, j * P, (j + 1) * P), prod[:, c, j, :], ident[:, :])
                mm.then_inc(s_f, 1)

            def up(e):
                if e >= 1:
                    eng.wait_ge(s_vl, 2 * e + 2)
                    eng.wait_ge(s_hp, 2 * e)
                    order = [(k, range(2)) for k in range(8)]
                else:
                    order = [(k, [c]) for c in range(2) for k in range(8)]
                for k, cs in order:
                    half = "A" if k < 4 else "B"
                    n = pos[("u" + half, e)]
                    if k % 4 == 0 and cs[0] == 0:
                        eng.wait_ge(s_L, n + 1)
                    if e == 0 and k == 0:
                        eng.wait_ge(s_vl, cs[0] + 1)
                    o = (k % 4) * I
                    gs, us = (n + 1) % NHL, (n + 2) % NHL
                    for c in cs:
                        ops = [(XH, HR, gs, 0), (XH, HR, us, 1), (XH, LR, gs, 0), (XH, LR, us, 1),
                               (XL, HR, gs, 0), (XL, HR, us, 1)]
                        for m, (X, Wt, s, g) in enumerate(ops):
                            mm = eng.matmul(bank(2 * c + g, 0, I), X[:, e % 2, c, k, :], Wt[:, s, o:o + I],
                                            start=(k == 0 and m < 2), stop=(k == 7 and m >= 4))
                    if k in (3, 7) and cs[-1] == 1:
                        mm.then_inc(s_k, 1)
                    if k == (1 if e else 7) and cs[-1] == 1 and e + 2 < E:
                        repeat(e + 2)

            def down(e):
                eng.wait_ge(s_fl, fq[("h", e, 1)] + 1)
                eng.wait_ge(s_L, pos[("dB", e)] + 1)
                for c in range(2):
                    for h in range(2):
                        o = 4 * e + 2 * c + h
                        if o >= 2:
                            eng.wait_ge(s_out, o - 1)
                        for j in range(3):
                            flat = j * D + h * 512
                            s = (pos[("dA", e)] + 2 + flat // UN) % NHL
                            f = flat % UN
                            for m, (X, Wt) in enumerate([(hH, HR), (hL, HR), (hH, LR)]):
                                mm = eng.matmul(bank(4 + h), X[:, c, j, :], Wt[:, s, f:f + 512],
                                                start=(j == 0 and m == 0), stop=(j == 2 and m == 2))
                        mm.then_inc(s_dn, 1)

            def turn_b(n):
                if n == 0:
                    eng.wait_ge(d_bw[4], 16)
                    eng.wait_ge(s_hp, 2 * E)
                    for q in range(8):
                        mm = eng.transpose(bank(0, q * NA, (q + 1) * NA), x1[0:NA, 2, q * P:(q + 1) * P],
                                           ident[0:NA, 0:NA])
                else:
                    j, f = divmod(n - 1, 2)
                    eng.wait_ge(d_bw[j % 4], 16 * (j // 4 + 1))
                    if n >= 4:
                        eng.wait_ge(s_bl, n - 2)
                    for r in range(4):
                        q = 4 * f + r
                        mm = eng.transpose(bank(n % 4, r * P, (r + 1) * P), x1[:, SB[j % 4], q * P:(q + 1) * P],
                                           ident[:, :])
                mm.then_inc(s_bf, 1)

            repeat(0)
            repeat(1)
            for e in range(E):
                up(e)
                if e >= 1:
                    down(e - 1)
                for c in range(2):
                    turn_h(e, c)
            for n in range(NB0):
                turn_b(n)
            down(E - 1)
            for n in range(NB0, 17):
                turn_b(n)

            eng.wait_ge(s_bl, 18)
            for k in range(9):
                eng.wait_ge(s_wl, k + 1)
                if k >= 2:
                    eng.wait_ge(s_ml, k - 1)
                if k == 1:
                    eng.wait_ge(s_out, 4 * E)
                if k == 8:
                    eng.wait_ge(s_fl, len(fq))
                    eng.wait_ge(s_arp, 1)
                    for f in range(2):
                        for r in range(4):
                            q = 4 * f + r
                            mm = eng.transpose(bank(6 + f, r * P, (r + 1) * P), arp[:, q * P:(q + 1) * P], ident[:, :])
                        mm.then_inc(s_at, 1)
                b0 = 3 * (k % 2)
                for q in range(8):
                    for m, (X, Y) in enumerate([(WH, BH), (WH, BL), (WL, BH)]):
                        for g, (a, z) in enumerate(CG):
                            mm = eng.matmul(bank(b0 + g, 0, z - a), X[:, k % 2, q, :], Y[:, q, a:z],
                                            start=(q == 0 and m == 0), stop=(q == 7 and m == 2))
                mm.then_inc(s_m, 1)


            def adapter(g):
                eng.wait_ge(s_xl, 4 * (g + 1))
                if g:
                    eng.wait_ge(s_xal, 2 * g)
                    eng.wait_ge(s_mtl, 2 * g - 1)
                else:
                    eng.wait_ge(s_atl, 2)
                for k in range(8):
                    for m, (X, Y) in enumerate([(ATH, xTH), (ATH, xTL), (ATL, xTH)]):
                        mm = eng.matmul(bank(7, 0, 256), X[:, k, :], Y[:, g % 2, k, :],
                                        start=(k == 0 and m == 0), stop=(k == 7 and m == 2))
                mm.then_inc(s_xa, 1)

            def turn_m(t):
                eng.wait_ge(s_mg, t + 1)
                eng.wait_ge(s_xal, 2 * min((t + 1) // 2 + 1, NB // 2))
                if t:
                    eng.wait_ge(s_mtl, t)
                eng.transpose(bank(7, 256, 384), mg[:, :], ident[:, :]).then_inc(s_mt, 1)

            def lora(t):
                eng.wait_ge(s_mtl, t + 1)
                if t == 0:
                    eng.wait_ge(s_lbl, 1)
                b0 = 3 * (t % 2)
                for m, (X, Y) in enumerate([(mgH, lbH), (mgH, lbL), (mgL, lbH)]):
                    for g, (a, z) in enumerate(CG):
                        z = min(z, D)
                        mm = eng.matmul(bank(b0 + g, 0, z - a), X[:, :], Y[:, a:z], start=False, stop=(m == 2),
                                        skip_group_check=True)
                mm.then_inc(s_lo, 1)

            for t in range(NB):
                g, o = t // 2, (t % 2) * P
                if t >= 2:
                    eng.wait_ge(s_fin, 2 * (t - 1))
                else:
                    eng.wait_ge(s_ml, 9)
                if t == 0:
                    eng.wait_ge(s_xl, 2)
                b0 = 3 * (t % 2)
                for k in range(9):
                    if t == 0 and k == 5:
                        adapter(0)
                    if k == 8:
                        eng.wait_ge(s_xal, 2 * (g + 1))
                        ops = [(xaH[:, g % 2, o:o + P], MH), (xaH[:, g % 2, o:o + P], ML), (xaL[:, g % 2, o:o + P], MH)]
                    else:
                        xh, xl = xTH[:, g % 2, k, o:o + P], xTL[:, g % 2, k, o:o + P]
                        ops = [(xh, MH), (xh, ML), (xl, MH)]
                    for m, (X, Y) in enumerate(ops):
                        for n, (a, z) in enumerate(CG):
                            mm = eng.matmul(bank(b0 + n, 0, z - a), X, Y[:, k, a:z],
                                            start=(k == 0 and m == 0), stop=(k == 8 and m == 2))
                    if k == 8:
                        mm.then_inc(s_mm, 1)
                    if k == 3 and t:
                        turn_m(t - 1)
                    if k == 6 and t:
                        lora(t - 1)
                if t % 2 and t + 1 < NB:
                    adapter(g + 1)
            turn_m(NB - 1)
            lora(NB - 1)

        @block.scalar
        def _(eng):
            def evac_y(i):
                if i >= NY:
                    eng.wait_ge(d_ys[i % NY], 16 * (i // NY))
                    eng.wait_ge(s_T, 2 * (i - NY) + 2)
                for h in range(2):
                    eng.wait_ge(s_Y, 2 * i + h + 1)
                    eng.activation(yrow[:, i % NY, :].rearrange("q (f j a) -> q f a j", f=4, j=8)[:, 2 * h:2 * h + 2],
                                   bank(h).rearrange("q (f a j) -> q f a j", f=2, j=8), ACT.Copy).then_inc(s_yr, 1)

            def store_y(i):
                eng.wait_ge(s_yr, 2 * i + 2)
                eng.dma_start(yd[i * P:(i + 1) * P, :], yrow[:, i % NY, :]).then_inc(d_ys[i % NY], 16)

            def copy_l(i):
                eng.wait_ge(s_lg, i + 1)
                if i >= 4:
                    eng.wait_ge(s_z, i - 3)
                eng.activation(lgs[:, i % 4, :], bank(4 + i % 2, 0, E), ACT.Copy).then_inc(s_lgc, 1)

            def exps(i):
                eng.wait_ge(s_z, i + 1)
                eng.activation(eb[:, i % 4, :], zz[:, i % 4, :], ACT.Exp).then_inc(s_e, 1)

            def copy_c(i):
                eng.wait_ge(s_cum, i + 1)
                if i >= 4:
                    eng.wait_ge(d_ts[i % 4], 16 * (i // 4))
                    eng.wait_ge(s_cb, i - 3)
                eng.activation(ct[:, i % 4, :], bank(6 + i % 2, 0, P, E), ACT.Copy)
                eng.activation(cb[:, i % 4, :], bank(6 + i % 2, P, P + E), ACT.Copy).then_inc(s_cte, 1)

            def store_c(i):
                eng.wait_ge(s_cte, i + 1)
                eng.dma_start(tab_v[i], ct[:, i % 4, :]).then_inc(d_ts[i % 4], 16)

            def store_w(i):
                eng.wait_ge(s_wy, i + 1)
                a = i - 3
                eng.dma_start(wdr[a * P:(i + 1) * P, :].rearrange("(b q) e -> q b e", q=P),
                              wy[:, a:i + 1, :]).then_inc(d_wy, 16)

            for i in range(NB + 8):
                if 3 <= i < NB + 3:
                    copy_l(i - 3)
                if 4 <= i < NB + 4:
                    exps(i - 4)
                if 5 <= i < NB + 5:
                    copy_c(i - 5)
                if i < NB:
                    evac_y(i)
                if 1 <= i <= NB:
                    store_y(i - 1)
                if 6 <= i < NB + 6:
                    store_c(i - 6)
                if i >= 8 and (i - 7) % 4 == 0:
                    store_w(i - 8)

            def split(k, e):
                n = pos[(k, e)]
                eng.wait_ge(d_raw[n % NRAW], 16 * (n // NRAW + 1))
                if n >= NHL:
                    wait_retired(eng, n - NHL)
                eng.activation(HR[:, (n + 2) % NHL, :], raw[:, n % NRAW, :], ACT.Copy).then_inc(s_H, 1)

            def high_x(e, c):
                eng.wait_ge(s_vt, 2 * e + c + 1)
                eng.activation(XH[:, e % 2, c, :, :].rearrange("p j (q t) -> p q j t", q=4), XR[:, c, :, :, :],
                               ACT.Copy).then_inc(s_vh, 1)

            def high_h(e, c):
                q = fq[("h", e, c)]
                eng.wait_ge(s_f, q + 1)
                eng.activation(hH[:, c, :, :], bank(6 + q % 2, 0, I), ACT.Copy).then_inc(s_fh, 1)

            def silu(e, c):
                eng.wait_ge(s_k, 2 * e + 2)
                if e:
                    eng.wait_ge(s_hp, 2 * (e - 1) + c + 1)
                eng.activation(sil[:, c, :], bank(2 * c, 0, I), ACT.Silu).then_inc(s_sl, 1)

            def result(e, c, h):
                if e:
                    eng.wait_ge(d_sc, 32 * e)
                eng.wait_ge(s_wc, e + 1)
                eng.wait_ge(s_dn, 4 * e + 2 * c + h + 1)
                eng.activation(ot[:, c, h * 512:(h + 1) * 512], bank(4 + h), ACT.Copy,
                               scale=wcol[:, c * E + e:c * E + e + 1]).then_inc(s_out, 1)

            for k in ("gA", "uA", "gB", "uB"):
                split(k, 0)
            for c in range(2):
                high_x(0, c)
            def high_b(n):
                eng.wait_ge(s_bf, n + 1)
                if n == 0:
                    eng.activation(BH[:, :, D:D + NA], bank(0, 0, 64).rearrange("p (q a) -> p q a", q=8), ACT.Copy)\
                       .then_inc(s_bh, 1)
                else:
                    j, f = divmod(n - 1, 2)
                    eng.activation(BH[:, 4 * f:4 * f + 4, j * P:(j + 1) * P],
                                   bank(n % 4).rearrange("p (q n) -> p q n", q=4), ACT.Copy).then_inc(s_bh, 1)

            for e in range(E + 1):
                if e >= 1:
                    high_h(e - 1, 0)
                    high_h(e - 1, 1)
                if e == E:
                    eng.wait_ge(s_k, 2 * E)
                    eng.wait_ge(d_la, 16 * 16)
                    eng.activation(BH[:, :, D + NA:NX], laR[:, :, :, :].rearrange("p q a r -> p q (a r)"), ACT.Copy)\
                       .then_inc(s_bh, 1)
                    for n in range(NB0):
                        high_b(n)
                if e + 1 < E:
                    split("gA", e + 1)
                    high_x(e + 1, 0)
                    split("uA", e + 1)
                    high_x(e + 1, 1)
                    split("gB", e + 1)
                    split("uB", e + 1)
                if e < E:
                    silu(e, 0)
                    silu(e, 1)
                    split("dA", e)
                if e >= 1:
                    result(e - 1, 0, 0)
                    result(e - 1, 0, 1)
                if e < E:
                    split("dB", e)
                if e >= 1:
                    result(e - 1, 1, 0)
                    result(e - 1, 1, 1)

            for n in range(NB0, 17):
                high_b(n)
            eng.wait_ge(s_dn, 4 * E)

            def high_w(k):
                if k < 8:
                    eng.wait_ge(d_wr[k % 2], 64 * (k // 2 + 1))
                    src = wr(k)
                else:
                    src = bmR[:, :, :, :].rearrange("p q a r -> p q (a r)")
                if k >= 2:
                    eng.wait_ge(s_m, k - 1)
                eng.activation(WH[:, k % 2, :, :], src, ACT.Copy).then_inc(s_wh, 1)

            def high_m(k):
                eng.wait_ge(s_m, k + 1)
                b0 = 3 * (k % 2)
                eng.activation(MH[:, k, 0:768].rearrange("p (g n) -> p g n", g=2), ps[:, b0:b0 + 2, 0:384], ACT.Copy)
                eng.activation(MH[:, k, 768:NX], bank(b0 + 2, 0, NX - 768), ACT.Copy).then_inc(s_mh, 1)

            high_w(0)
            high_w(1)
            eng.wait_ge(d_sc, 32 * E)
            for k in range(9):
                high_m(k)
                if k + 2 < 9:
                    high_w(k + 2)

            eng.wait_ge(d_ab, 32)
            for f in range(2):
                eng.wait_ge(s_at, f + 1)
                eng.activation(ATH[:, 4 * f:4 * f + 4, :], bank(6 + f), ACT.Copy).then_inc(s_ath, 1)

            def high_r(t):
                g, o = t // 2, (t % 2) * P
                eng.wait_ge(s_xr, t + 1)
                if t >= 4:
                    eng.wait_ge(s_mm, t - 3)
                eng.activation(xTH[:, g % 2, :, o:o + P].rearrange("p j (q t) -> p q j t", q=4), xr[:, t % 2, :, :, :],
                               ACT.Copy).then_inc(s_xh, 2)

            def high_a(g):
                eng.wait_ge(s_xa, g + 1)
                for o in range(2):
                    b = 2 * g + o
                    eng.activation(xaH[:, g % 2, o * P:(o + 1) * P], bank(7, o * P, (o + 1) * P), ACT.Copy,
                                   scale=mk[:, b:b + 1]).then_inc(s_xah, 1)

            def exp2(t):
                eng.wait_ge(s_z2, t + 1)
                if t >= 2:
                    eng.wait_ge(s_mg, t - 1)
                eng.activation(e2[:, t % 2, :], z2[:, 0:NA], ACT.Exp).then_inc(s_e2, 1)

            def high_g(t):
                eng.wait_ge(s_mt, t + 1)
                if t:
                    eng.wait_ge(s_lo, t)
                eng.activation(mgH[:, :], bank(7, 256, 384), ACT.Copy).then_inc(s_mth, 1)

            eng.wait_ge(d_ab, 32)
            high_r(0)
            high_r(1)
            eng.activation(lbH[:, :], lb, ACT.Copy).then_inc(s_lbh, 1)
            high_a(0)
            for t in range(NB):
                if t:
                    exp2(t - 1)
                if t + 2 < NB:
                    high_r(t + 2)
                if t:
                    high_g(t - 1)
                if t % 2 and t + 1 < NB:
                    high_a(t // 2 + 1)
            exp2(NB - 1)
            high_g(NB - 1)

        @block.vector
        def _(eng):
            ch = Count(eng, s_dv)
            eng.memset(zrow[:, :], 0.0).then_inc(s_zr, 1)
            eng.memset(gT[:, :, :], 0.0)
            eng.memset(tacc[:, :, :], 0.0)
            ch.link(eng.memset(qm[:, :, :], 0.0))
            for q in range(4):
                eng.memset(f4[32 * q:32 * q + 32, :], float(q))
                eng.memset(qm[32 * q:32 * q + 32, q, :], 1.0)
            ch.link(eng.memset(sm[:, :], 0.0))
            eng.wait_ge(d_small, 16)
            eng.wait_ge(s_cst, 1)
            eng.tensor_scalar(cidx[:, :], condi[:, :], float(P), pf[:, 0:1], ALU.mult, ALU.add).then_inc(s_cidx, 1)
            eng.wait_ge(d_gw, 16)
            for f in range(4):
                mm = eng.tensor_copy(gwp.rearrange("e (f j a) -> e f j a", f=4, j=8)[:, f],
                                     gw.rearrange("e (f a j) -> e f j a", f=4, j=8)[:, f])
            mm.then_inc(s_gwp, 1)
            eng.wait_ge(s_gt, 1)
            eng.tensor_copy(gT[:, :, 0:E], bank(4).rearrange("p (k e) -> p k e", k=8)).then_inc(s_gte, 1)
            eng.wait_ge(d_bc, 16 * 9)
            ch.link(eng.tensor_scalar(mkt[:, 0, :], adi[:, :], -float(R), pf[:, 0:1], ALU.mult, ALU.add))
            ch.link(eng.tensor_scalar(mkt[:, 1, :], mkt[:, 0, :], 0.0, scp[:, 0:1], ALU.is_ge, ALU.mult))
            eng.scalar_tensor_tensor(mk[:, :], mkt[:, 0, :], R - 0.5, mkt[:, 1, :], ALU.is_le, ALU.mult)

            def evac_t(i, f):
                eng.wait_ge(s_T, 2 * i + f + 1)
                if i >= 2:
                    eng.wait_ge(s_lg, i - 1)
                eng.tensor_copy(yT[:, i % 2, 4 * f:4 * f + 4, :], bank(2 + f)).then_inc(s_yT, 1)

            seen = {}

            def top(i):
                eng.wait_ge(s_lgc, i + 1)
                seen["m", i] = ch.mark(eng.max(m8[:, i % 4, :], lgs[:, i % 4, :]))

            def shift(i):
                eng.wait_ge(s_dv, seen["m", i])
                b = i % 4
                eng.tensor_scalar(z8[:, b, :], m8[:, b, :], m8[:, b, 0:1], ZMIN, ALU.subtract, ALU.max)
                eng.tensor_scalar(zz[:, b, :], lgs[:, b, :], m8[:, b, 0:1], ZMIN, ALU.subtract, ALU.max)\
                   .then_inc(s_z, 1)

            def choose(i):
                eng.wait_ge(s_z, i + 1)
                b = i % 4
                seen["r", i] = ch.mark(eng.match_replace(zr[:, b, :], z8[:, b, :], zz[:, b, :], 1.0))

            def marks(i):
                eng.wait_ge(s_dv, seen["r", i])
                b = i % 4
                if i >= 4:
                    eng.wait_ge(s_cum, i - 2)
                eng.tensor_scalar(mask[:, b, :], zr[:, b, :], 0.5, None, ALU.is_ge).then_inc(s_mask, 1)
                if i:
                    eng.wait_ge(s_mask, 2 * i)
                    eng.scalar_tensor_tensor(macc[:, b, :], zr[:, b, :], 0.5, macc[:, (i - 1) % 4, :],
                                             ALU.is_ge, ALU.add).then_inc(s_mask, 1)
                else:
                    eng.tensor_scalar(macc[:, 0, :], zr[:, 0, :], 0.5, None, ALU.is_ge).then_inc(s_mask, 1)

            def weigh(i):
                b = i % 4
                eng.wait_ge(s_e, i + 1)
                seen["w", i] = ch.mark(eng.scalar_tensor_tensor(
                    wm[:, b, :], zr[:, b, :], 0.5, eb[:, b, :], ALU.is_ge, ALU.mult, accum_out=sm[:, b:b + 1]))

            def invert(i):
                eng.wait_ge(s_dv, seen["w", i])
                b = i % 4
                seen["c", i] = ch.mark(eng.reciprocal(rc[:, b:b + 1], sm[:, b:b + 1]))

            def share(i):
                eng.wait_ge(s_dv, seen["c", i])
                b = i % 4
                eng.tensor_scalar(wy[:, i, :], wm[:, b, :], rc[:, b:b + 1], None, ALU.mult).then_inc(s_wy, 1)

            def tiles(i):
                eng.wait_ge(s_cte, i + 1)
                if i:
                    eng.wait_ge(s_cb, i)
                eng.scalar_tensor_tensor(tacc[:, 0, :], cb[:, i % 4, :], slot[:, 0:1], tacc[:, 0, :],
                                         ALU.is_le, ALU.add)
                eng.scalar_tensor_tensor(tacc[:, 1, :], cb[:, i % 4, :], slot[:, 1:2], tacc[:, 1, :],
                                         ALU.is_le, ALU.add).then_inc(s_cb, 1)

            for i in range(NB + 8):
                a = i - 3
                if 0 <= a < NB:
                    top(a)
                if 1 <= i <= NB:
                    evac_t(i - 1, 0)
                if 0 <= a < NB:
                    shift(a)
                if 0 <= i - 6 < NB:
                    tiles(i - 6)
                if 0 <= a - 1 < NB:
                    weigh(a - 1)
                if 0 <= a < NB:
                    choose(a)
                if 0 <= a - 1 < NB:
                    invert(a - 1)
                if 1 <= i <= NB:
                    evac_t(i - 1, 1)
                if 0 <= a < NB:
                    marks(a)
                if 0 <= a - 1 < NB:
                    share(a - 1)
            eng.wait_ge(s_cb, NB)
            eng.tensor_scalar(t128[:, :, :], tacc[:, :, :], float(P), None, ALU.mult)
            ch.link(eng.tensor_tensor(rowi[:, :].rearrange("p (c e) -> p c e", c=2), tacc[:, :, :], e32[:, :, :],
                                      ALU.add))
            eng.engine_nop().then_inc(s_idx, 1)

            def split(k, e):
                n = pos[(k, e)]
                eng.wait_ge(s_H, n + 1)
                eng.tensor_tensor(LR[:, (n + 2) % NHL, :], raw[:, n % NRAW, :], HR[:, (n + 2) % NHL, :].bitcast(F32),
                                  ALU.subtract).then_inc(s_L, 1)

            def turn_x(e, c):
                eng.wait_ge(d_xg[c], 64 * (e + 1))
                if e:
                    eng.wait_ge(s_vl, 2 * (e - 1) + c + 1)
                eng.transpose(XR[:, c, :, :, :].rearrange("p q j t -> p (q j t)"),
                              Xg[:, c, :, :].rearrange("p q s -> p (q s)")).then_inc(s_vt, 1)

            def low_x(e, c):
                eng.wait_ge(s_vh, 2 * e + c + 1)
                eng.tensor_tensor(XL[:, e % 2, c, :, :].rearrange("p j (q t) -> p q j t", q=4), XR[:, c, :, :, :],
                                  XH[:, e % 2, c, :, :].rearrange("p j (q t) -> p q j t", q=4).bitcast(F32),
                                  ALU.subtract).then_inc(s_vl, 1)

            def index(e):
                q = fq[("i", e)]
                eng.wait_ge(s_f, q + 1)
                eng.tensor_scalar(idx4[:, e % 4, :], bank(6 + q % 2, 0, 8), 4.0, f4[:, 0:1], ALU.mult, ALU.add)\
                   .then_inc(s_i4, 1)
                eng.wait_ge(s_i4, e + 1)
                eng.engine_nop().then_inc(s_fl, 1)

            def low_h(e, c):
                q = fq[("h", e, c)]
                eng.wait_ge(s_fh, 2 * e + c + 1)
                eng.tensor_tensor(hL[:, c, :, :].rearrange("p k n -> p (k n)"), bank(6 + q % 2, 0, I),
                                  hH[:, c, :, :].rearrange("p k n -> p (k n)").bitcast(F32),
                                  ALU.subtract).then_inc(s_fl, 1)

            def product(e, c):
                eng.wait_ge(s_sl, 2 * e + c + 1)
                if e:
                    eng.wait_ge(s_f, fq[("h", e - 1, c)] + 1)
                eng.tensor_tensor(prod[:, c, :, :].rearrange("q j p -> q p j"),
                                  sil[:, c, :].rearrange("q (p j) -> q p j", j=3),
                                  bank(2 * c + 1, 0, I).rearrange("q (p j) -> q p j", j=3),
                                  ALU.mult).then_inc(s_hp, 1)

            def token(e):
                eng.wait_ge(d_g[e % 2], 32 * (e // 2 + 1))
                for c in range(2):
                    ins = eng.tensor_scalar(Gj[:, c, :], G[:, e % 2, c, :], slot[:, c:c + 1], None,
                                            ALU.is_le, ALU.add, accum_out=cnt[:, c:c + 1])
                    n = ch.mark(ins)
                eng.wait_ge(s_dv, n)
                for c in range(2):
                    n = ch.mark(eng.tensor_scalar(tokf[:, e % 4, c:c + 1], t128[:, c, e:e + 1], cnt[:, c:c + 1],
                                                  dum[:, c:c + 1], ALU.add, ALU.min))
                eng.wait_ge(s_dv, n)
                eng.tensor_copy(toki[:, :].rearrange("p (c e) -> p c e", c=2)[:, :, e], tokf[:, e % 4, :])
                eng.tensor_tensor(tokq[:, e % 4, :].rearrange("p (q c) -> p q c", q=4), qm[:, :, :],
                                  tokf[:, e % 4, :].unsqueeze(1).to_broadcast([P, 4, 2]), ALU.mult)\
                   .then_inc(s_tok, 2)

            def column(e):
                eng.wait_ge(d_wg[e % 2], 32 * (e // 2 + 1))
                eng.tensor_copy(wcol[:, :].rearrange("p (c e) -> p c e", c=2)[:, :, e], Wg[:, e % 2, :, e])\
                   .then_inc(s_wc, 1)

            split("gA", 0)
            split("uA", 0)
            token(0)
            index(0)
            split("gB", 0)
            token(1)
            index(1)
            split("uB", 0)
            for c in range(2):
                turn_x(0, c)
                low_x(0, c)
            for e in range(E + 1):
                if e >= 1:
                    low_h(e - 1, 0)
                    low_h(e - 1, 1)
                if e >= 1 and e + 2 < E:
                    index(e + 2)
                if e + 1 < E:
                    turn_x(e + 1, 0)
                    turn_x(e + 1, 1)
                    split("gA", e + 1)
                    low_x(e + 1, 0)
                    split("uA", e + 1)
                    low_x(e + 1, 1)
                    split("gB", e + 1)
                    split("uB", e + 1)
                    if e == 0:
                        column(0)
                    column(e + 1)
                if e == 0:
                    token(2)
                    index(2)
                if e < E:
                    product(e, 0)
                    product(e, 1)
                    split("dA", e)
                if e + 3 < E:
                    token(e + 3)
                if e < E:
                    split("dB", e)

            eng.wait_ge(s_k, 2 * E)
            eng.wait_ge(s_bh, 1)
            eng.tensor_tensor(BL[:, :, D + NA:NX], laR[:, :, :, :].rearrange("p q a r -> p q (a r)"),
                              BH[:, :, D + NA:NX].bitcast(F32), ALU.subtract).then_inc(s_bl, 1)
            for n in range(17):
                eng.wait_ge(s_bh, n + 2)
                if n == 0:
                    ins = eng.tensor_tensor(BL[:, :, D:D + NA], bank(0, 0, 64).rearrange("p (q a) -> p q a", q=8),
                                            BH[:, :, D:D + NA].bitcast(F32), ALU.subtract)
                else:
                    j, f = divmod(n - 1, 2)
                    a = (slice(None), slice(4 * f, 4 * f + 4), slice(j * P, (j + 1) * P))
                    ins = eng.tensor_tensor(BL[a], bank(n % 4).rearrange("p (q n) -> p q n", q=4),
                                            BH[a].bitcast(F32), ALU.subtract)
                ins.then_inc(s_bl, 1)

            def low_w(k):
                eng.wait_ge(s_wh, k + 1)
                src = wr(k) if k < 8 else bmR[:, :, :, :].rearrange("p q a r -> p q (a r)")
                eng.tensor_tensor(WL[:, k % 2, :, :], src, WH[:, k % 2, :, :].bitcast(F32), ALU.subtract)\
                   .then_inc(s_wl, 1)

            def turn_r(t):
                eng.wait_ge(d_xq[t % 2], 64 * (t // 2 + 1))
                eng.transpose(xr[:, t % 2, :, :, :].rearrange("p q j t -> p (q j t)"),
                              xq(t)).then_inc(s_xr, 1)

            def low_m(k):
                eng.wait_ge(s_mh, k + 1)
                b0 = 3 * (k % 2)
                eng.tensor_tensor(ML[:, k, 0:768].rearrange("p (g n) -> p g n", g=2), ps[:, b0:b0 + 2, 0:384],
                                  MH[:, k, 0:768].rearrange("p (g n) -> p g n", g=2).bitcast(F32), ALU.subtract)
                eng.tensor_tensor(ML[:, k, 768:NX], bank(b0 + 2, 0, NX - 768), MH[:, k, 768:NX].bitcast(F32),
                                  ALU.subtract).then_inc(s_ml, 1)

            eng.wait_ge(s_dn, 4 * E)
            low_w(0)
            low_w(1)
            for k in range(9):
                if k == 8:
                    eng.wait_ge(s_m, 9)
                    turn_r(0)
                low_m(k)
                if k + 2 < 9:
                    low_w(k + 2)
                if k == 6:
                    eng.wait_ge(d_ab, 32)
                    eng.wait_ge(s_wl, 8)
                    for f in range(4):
                        mm = eng.tensor_copy(arp.rearrange("p (j f i) -> p f j i", f=4, j=8)[:, f],
                                             ar.rearrange("p (f j i) -> p f j i", f=4, j=8)[:, f])
                    mm.then_inc(s_arp, 1)

            eng.memset(z2[:, 8:14], 1e30).then_inc(s_pad, 1)
            for f in range(2):
                eng.wait_ge(s_ath, f + 1)
                eng.tensor_tensor(ATL[:, 4 * f:4 * f + 4, :].rearrange("p k n -> p (k n)"), bank(6 + f),
                                  ATH[:, 4 * f:4 * f + 4, :].rearrange("p k n -> p (k n)").bitcast(F32),
                                  ALU.subtract).then_inc(s_atl, 1)

            def low_r(t):
                g, o = t // 2, (t % 2) * P
                eng.wait_ge(s_xh, 2 * t + 2)
                a = (slice(None), g % 2, slice(None), slice(o, o + P))
                if t >= 4:
                    eng.wait_ge(s_mm, t - 3)
                eng.tensor_tensor(xTL[a].rearrange("p j (q t) -> p q j t", q=4), xr[:, t % 2, :, :, :],
                                  xTH[a].rearrange("p j (q t) -> p q j t", q=4).bitcast(F32),
                                  ALU.subtract).then_inc(s_xl, 2)

            def low_a(g):
                for o in range(2):
                    b = 2 * g + o
                    eng.wait_ge(s_xah, 2 * g + 2)
                    a = (slice(None), g % 2, slice(o * P, (o + 1) * P))
                    eng.scalar_tensor_tensor(xaL[a], bank(7, o * P, (o + 1) * P), mk[:, b:b + 1], xaH[a].bitcast(F32),
                                             ALU.mult, ALU.subtract).then_inc(s_xal, 1)

            def gate_of(t):
                b2 = 3 * (t % 2) + 2
                eng.wait_ge(s_mm, t + 1)
                if t == 0:
                    eng.wait_ge(d_bi, 32)
                    eng.wait_ge(s_pad, 1)
                ch.link(eng.tensor_tensor(lg2[:, :], bank(b2, 256, 264), rb[:, :], ALU.add))
                ch.link(eng.tensor_reduce(mx2[:, :], lg2[:, :], AX_X, ALU.max))
                if t:
                    eng.wait_ge(s_e2, t)
                ch.link(eng.tensor_scalar(z2[:, 0:NA], lg2[:, :], mx2[:, 0:1], ZMIN, ALU.subtract, ALU.max))
                eng.engine_nop().then_inc(s_z2, 1)
                ch.link(eng.max(t8[:, :], z2[:, :]))
                ch.link(eng.match_replace(zr2[:, :], t8[:, :], z2[:, :], 1.0))
                eng.wait_ge(s_e2, t + 1)
                ch.link(eng.scalar_tensor_tensor(g2[:, :], zr2[:, 0:NA], 0.5, e2[:, t % 2, :], ALU.is_ge, ALU.mult,
                                                 accum_out=sm2[:, 0:1]))
                ch.link(eng.reciprocal(sm2[:, 1:2], sm2[:, 0:1]))
                ch.link(eng.tensor_scalar(gate[:, :], g2[:, :], sm2[:, 1:2], 2.0, ALU.mult, ALU.mult))
                if t:
                    eng.wait_ge(s_mt, t)
                eng.tensor_tensor(mg[:, :].rearrange("p (a r) -> p a r", a=NA),
                                  bank(b2, 264, 392).rearrange("p (a r) -> p a r", a=NA),
                                  gate[:, :].unsqueeze(2).to_broadcast([P, NA, R]), ALU.mult).then_inc(s_mg, 1)

            def low_g(t):
                eng.wait_ge(s_mth, t + 1)
                eng.tensor_tensor(mgL[:, :], bank(7, 256, 384), mgH[:, :].bitcast(F32), ALU.subtract)\
                   .then_inc(s_mtl, 1)

            def final(t):
                b0, s = 3 * (t % 2), t % 6
                eng.wait_ge(s_lo, t + 1)
                eng.wait_ge(s_pb, t + 1)
                if t >= 3:
                    eng.wait_ge(d_o[t % 3], 16 * (t // 3))
                eng.tensor_tensor(osb[:, t % 3, 0:768].rearrange("p (g n) -> p g n", g=2), ps[:, b0:b0 + 2, 0:384],
                                  x1[:, s, 0:768].rearrange("p (g n) -> p g n", g=2), ALU.add).then_inc(s_fin, 1)
                eng.tensor_tensor(osb[:, t % 3, 768:D], bank(b0 + 2, 0, 256), x1[:, s, 768:D],
                                  ALU.add).then_inc(s_fin, 1)

            low_r(0)
            turn_r(1)
            low_r(1)
            eng.wait_ge(s_lbh, 1)
            eng.tensor_tensor(lbL[:, :], lb, lbH[:, :].bitcast(F32), ALU.subtract).then_inc(s_lbl, 1)
            low_a(0)
            turn_r(2)
            for t in range(NB):
                if t:
                    gate_of(t - 1)
                if t:
                    low_g(t - 1)
                if t + 2 < NB:
                    low_r(t + 2)
                if t:
                    final(t - 1)
                if t + 3 < NB:
                    turn_r(t + 3)
                if t % 2 and t + 1 < NB:
                    low_a(t // 2 + 1)
            gate_of(NB - 1)
            low_g(NB - 1)
            final(NB - 1)


_INS = ["x", "itok_B_1_198", "itok_B_0_6", "L0_cond_weights", "L0_ffn_gate_w", "L0_ffn_wg", "L0_ffn_wu", "L0_ffn_wd",
        "L1_cond_W", "L1_cond_A", "L1_cond_Bm", "L1_cond_scalings", "L1_ffn_base_w", "L1_ffn_base_b",
        "L1_ffn_router_w", "L1_ffn_router_b", "L1_ffn_lora_A", "L1_ffn_lora_B"]


def kernel(**inputs):
    import numpy as _np
    import concourse.bacc as _bacc
    from concourse import mybir as _mybir
    from concourse.bass_utils import run_bass_kernel_spmd as _run

    nc = _bacc.Bacc("TRN2", target_bir_lowering=False, num_devices=1)
    arrays, args = {}, []
    for name in _INS:
        a = _np.ascontiguousarray(inputs[name])
        arrays[f"in_{name}"] = a
        args.append(nc.dram_tensor(f"in_{name}", a.shape, _mybir.dt.from_np(a.dtype), kind="ExternalInput").ap())
    o = nc.dram_tensor("out_0", (32, 128, 1024), _mybir.dt.float32, kind="ExternalOutput").ap()
    adaln_ffn_kernel(nc, *args, o)
    r = _run(nc, [arrays], core_ids=[0])
    return r.results[0]["out_0"]
```
